# Optimizing a Trainium2 kernel written in Bass

```python
import numpy as np
import jax
import jax.numpy as jnp

def _softmax(x, axis=-1):
    return jax.nn.softmax(x, axis=axis)

def _gelu(x):
    return jax.nn.gelu(x, approximate=True)

def _silu(x):
    return jax.nn.silu(x)

def _sigmoid(x):
    return jax.nn.sigmoid(x)

def _layernorm(x, axis=-1, eps=1e-05):
    m = jnp.mean(x, axis=axis, keepdims=True)
    v = jnp.var(x, axis=axis, keepdims=True)
    return (x - m) / jnp.sqrt(v + eps)

def _scatter_add(tgt, idx, src, axis=0):
    return tgt.at[idx].add(src)

def _segment_sum(src, seg, n):
    return jax.ops.segment_sum(src, seg, n)
kernel_name = 'mk_recurrent_d1_jaxref_r4_6749d9'

def setup_inputs(seed: int=0):
    np.random.seed(seed)
    _w = jnp.asarray

    def _L0_attn_setup():
        import jax, jax.numpy as jnp
        import numpy as np
        D_MODEL = 512
        N_HEADS = 16
        HEAD_DIM = D_MODEL // N_HEADS
        SCALE = HEAD_DIM ** (-0.5)
        key = jax.random.key(seed)
        ks = jax.random.split(key, 9)
        B, L, D = (4, 1024, D_MODEL)
        s = 1.0 / np.sqrt(D)
        inp = {'x': jax.random.normal(ks[0], (B, L, D), dtype=jnp.float32)}
        inp['Wq'] = jax.random.normal(ks[1], (D, D), dtype=jnp.float32) * s
        inp['bq'] = jnp.zeros((D,), dtype=jnp.float32)
        inp['Wk'] = jax.random.normal(ks[2], (D, D), dtype=jnp.float32) * s
        inp['bk'] = jnp.zeros((D,), dtype=jnp.float32)
        inp['Wv'] = jax.random.normal(ks[3], (D, D), dtype=jnp.float32) * s
        inp['bv'] = jnp.zeros((D,), dtype=jnp.float32)
        inp['Wo'] = jax.random.normal(ks[4], (D, D), dtype=jnp.float32) * s
        inp['bo'] = jnp.zeros((D,), dtype=jnp.float32)
        return inp
    _L0_attn_in = _L0_attn_setup()

    def _L0_ffn_setup():
        import jax, jax.numpy as jnp
        import numpy as np
        HIDDEN = 512
        INTER = 2048
        SCALE = 64.0

        def fwht(x):
            orig_shape = x.shape
            n = orig_shape[-1]
            x = x.reshape(-1, n)
            h = 1
            while h < n:
                x = x.reshape(-1, n // (2 * h), 2, h)
                a, b = (x[:, :, 0, :], x[:, :, 1, :])
                x = jnp.stack([a + b, a - b], axis=2).reshape(-1, n)
                h *= 2
            return (x / jnp.sqrt(jnp.asarray(n, x.dtype))).reshape(orig_shape)
        key = jax.random.key(seed)
        ks = jax.random.split(key, 8)
        inp = jax.random.normal(ks[0], (4, 512, HIDDEN), dtype=jnp.float32)
        SU_ug = jnp.where(jax.random.bernoulli(ks[1], 0.5, (HIDDEN,)), 1.0, -1.0).astype(jnp.float32)
        SU_dp = jnp.where(jax.random.bernoulli(ks[2], 0.5, (INTER,)), 1.0, -1.0).astype(jnp.float32)
        Wscale_ug = jax.random.uniform(ks[3], (2 * INTER,), jnp.float32, 0.5, 1.5)
        Wscale_dp = jax.random.uniform(ks[4], (HIDDEN,), jnp.float32, 0.5, 1.5)
        W_up = jax.random.normal(ks[5], (INTER, HIDDEN), dtype=jnp.float32) * 0.02
        W_gate = jax.random.normal(ks[6], (INTER, HIDDEN), dtype=jnp.float32) * 0.02
        W_down = jax.random.normal(ks[7], (HIDDEN, INTER), dtype=jnp.float32) * 0.02
        return {'input': inp, 'SU_ug': SU_ug, 'SU_dp': SU_dp, 'Wscale_ug': Wscale_ug, 'Wscale_dp': Wscale_dp, 'W_up': W_up, 'W_gate': W_gate, 'W_down': W_down}
    _L0_ffn_in = _L0_ffn_setup()
    _d = {'L0_attn_x': _L0_attn_in['x'], 'L0_attn_Wq': _L0_attn_in['Wq'], 'L0_attn_bq': _L0_attn_in['bq'], 'L0_attn_Wk': _L0_attn_in['Wk'], 'L0_attn_bk': _L0_attn_in['bk'], 'L0_attn_Wv': _L0_attn_in['Wv'], 'L0_attn_bv': _L0_attn_in['bv'], 'L0_attn_Wo': _L0_attn_in['Wo'], 'L0_attn_bo': _L0_attn_in['bo'], 'L0_ffn_SU_ug': _L0_ffn_in['SU_ug'], 'L0_ffn_SU_dp': _L0_ffn_in['SU_dp'], 'L0_ffn_Wscale_ug': _L0_ffn_in['Wscale_ug'], 'L0_ffn_Wscale_dp': _L0_ffn_in['Wscale_dp'], 'L0_ffn_W_up': _L0_ffn_in['W_up'], 'L0_ffn_W_gate': _L0_ffn_in['W_gate'], 'L0_ffn_W_down': _L0_ffn_in['W_down']}
    _x0 = _d['L0_attn_x']
    _d['L0_attn_x'] = jax.random.normal(jax.random.fold_in(jax.random.key(seed), 1), (8, 512, 512), dtype=_x0.dtype)
    del _x0
    return _d

def reference(L0_attn_x, L0_attn_Wq, L0_attn_bq, L0_attn_Wk, L0_attn_bk, L0_attn_Wv, L0_attn_bv, L0_attn_Wo, L0_attn_bo, L0_ffn_SU_ug, L0_ffn_SU_dp, L0_ffn_Wscale_ug, L0_ffn_Wscale_dp, L0_ffn_W_up, L0_ffn_W_gate, L0_ffn_W_down):

    def _L0_attn_ref(x, Wq, bq, Wk, bk, Wv, bv, Wo, bo):
        import jax, jax.numpy as jnp
        import numpy as np
        D_MODEL = 512
        N_HEADS = 16
        HEAD_DIM = D_MODEL // N_HEADS
        SCALE = HEAD_DIM ** (-0.5)
        B, L, D = x.shape
        H, Hd = (N_HEADS, HEAD_DIM)
        q = jnp.einsum('bld,ed->ble', x, Wq) + bq
        k = jnp.einsum('bld,ed->ble', x, Wk) + bk
        v = jnp.einsum('bld,ed->ble', x, Wv) + bv
        phi_q = jax.nn.elu(q) + 1.0
        phi_k = jax.nn.elu(k) + 1.0
        phi_q = phi_q.reshape(B, L, H, Hd)
        phi_k = phi_k.reshape(B, L, H, Hd)
        v = v.reshape(B, L, H, Hd)
        kv_sum = jnp.cumsum(phi_k * v, axis=1)
        context = (phi_q * kv_sum).reshape(B, L, D) * SCALE
        return jnp.einsum('bld,ed->ble', context, Wo) + bo

    def _L0_ffn_ref(input, SU_ug, SU_dp, Wscale_ug, Wscale_dp, W_up, W_gate, W_down):
        import jax, jax.numpy as jnp
        import numpy as np
        HIDDEN = 512
        INTER = 2048
        SCALE = 64.0

        def fwht(x):
            orig_shape = x.shape
            n = orig_shape[-1]
            x = x.reshape(-1, n)
            h = 1
            while h < n:
                x = x.reshape(-1, n // (2 * h), 2, h)
                a, b = (x[:, :, 0, :], x[:, :, 1, :])
                x = jnp.stack([a + b, a - b], axis=2).reshape(-1, n)
                h *= 2
            return (x / jnp.sqrt(jnp.asarray(n, x.dtype))).reshape(orig_shape)
        n = SU_ug.shape[0]
        x = input.reshape(-1, n)
        x = fwht(x * SU_ug) / SCALE
        x_up = x @ W_up.T * (Wscale_ug[:INTER] * SCALE)
        x_gate = x @ W_gate.T * (Wscale_ug[INTER:] * SCALE)
        x = jax.nn.silu(x_gate) * x_up
        x = fwht(x * SU_dp) / SCALE
        x = x @ W_down.T * (Wscale_dp * SCALE)
        return x.reshape(input.shape)
    x = L0_attn_x
    xn = _layernorm(x, axis=-1)
    s = _L0_attn_ref(xn, L0_attn_Wq, L0_attn_bq, L0_attn_Wk, L0_attn_bk, L0_attn_Wv, L0_attn_bv, L0_attn_Wo, L0_attn_bo)
    g = _silu(_L0_ffn_ref(xn, L0_ffn_SU_ug, L0_ffn_SU_dp, L0_ffn_Wscale_ug, L0_ffn_Wscale_dp, L0_ffn_W_up, L0_ffn_W_gate, L0_ffn_W_down))
    x = x + s * g
    return x

_drawn_inputs = setup_inputs


def setup_inputs(seed=0):
    import zlib

    import numpy as np

    out = dict(_drawn_inputs(seed))
    spreads = {'L0_attn_bq': (0.0, 0.305),
     'L0_attn_bk': (0.0, 0.281),
     'L0_attn_bv': (0.0, 0.1),
     'L0_attn_bo': (0.0, 0.8)}
    factors = {}
    for name, (base, spread) in spreads.items():
        noise = np.random.default_rng([zlib.crc32(name.encode()), seed]).standard_normal(out[name].shape)
        drawn = base * np.exp(spread * noise) if base else spread * noise
        out[name] = jnp.asarray(drawn.astype(out[name].dtype))
    for name, factor in factors.items():
        out[name] = (out[name] * factor).astype(out[name].dtype)
    return out
```

```python
from contextlib import ExitStack

import concourse.bass as bass
from concourse import mybir

F32 = mybir.dt.float32
F16 = mybir.dt.float16
BF16 = mybir.dt.bfloat16
I32 = mybir.dt.int32
ALU = mybir.AluOpType
ACT = mybir.ActivationFunctionType
AX_X = mybir.AxisListType.X
REDUCE_MAX = bass.bass_isa.ReduceOp.max

P = 128
CHUNKS, T, D = 8, 512, 512
F = 2048
HEAD_DIM = D // 16
KB = D // P
TB = T // P
NI = F // P
BLOCKS = F // 512
EPS = 1e-5

X_SCALE = 1024.0
TOP = 14
TINY_SQUARE = 2.0 ** -120
TINY = 27
EXPONENT = 0x7F800000

BK, BV, BQ, SU_UG, SU_DP, WS_GATE, WS_UP = 0, 4, 8, 12, 16, 32, 48
VECS = 64
K, V, Q, O = range(4)
M_SU, M_GATE, M_UP, M_DOWN, M_COEF = range(4, 9)
MAXIMA = 9
GATE, UP = 0, 1
UNITS = [(b, m) for b in range(BLOCKS) for m in (GATE, UP)] + [(g, None) for g in range(NI // KB)]
UG_UNITS = 2 * BLOCKS
ROOTS = 2 * NI + KB
MARGIN = 1.02
HI, LO = 0, 1


def build(nc, x, wk_t, wv_t, wq_t, wo_t, gate_t, up_t, down_t, vecs, rows, ident_in, hada_in, out):
    with ExitStack() as ctx:
        def sb(name, shape, dt=F32):
            return ctx.enter_context(nc.sbuf_tensor(name, shape, dt))

        def sem(name):
            return ctx.enter_context(nc.semaphore(name))

        w_attn = sb("w_attn", [P, 4, 2, KB, D], F16)
        w_ug = sb("w_ug", [P, 2 * BLOCKS * KB * 512])
        w_down = sb("w_down", [P, NI * D])
        ug_raw = w_ug[:, :].rearrange("p (m b k n) -> p m b k n", m=2, b=BLOCKS, k=KB)
        ug = w_ug[:, :].bitcast(F16).rearrange("p (m b k s n) -> p m b k s n", m=2, b=BLOCKS, k=KB, s=2)
        down_raw = w_down[:, :].rearrange("p (k n) -> p k n", k=NI)
        down = w_down[:, :].bitcast(F16).rearrange("p (k s n) -> p k s n", k=NI, s=2)

        x_ln = sb("x_ln", [P, TB, D])
        x_res = sb("x_res", [P, TB, D])
        xt = sb("xt", [P, 2, KB, T], F16)
        e_k, r_k = sb("e_k", [P, T]), sb("r_k", [P, T])
        e_q, r_q = sb("e_q", [P, T]), sb("r_q", [P, T])
        v_sb = sb("v_sb", [P, T])
        ctx_f = sb("ctx_f", [P, KB, T])
        ctx_s = sb("ctx_s", [P, 2, KB, T], F16)
        scratch = sb("scratch", [P, 4096])
        silu = scratch[:, 0:1024].rearrange("p (r n) -> p r n", r=2)
        gate_g = scratch[:, 1024:2048].rearrange("p (r n) -> p r n", r=2)
        h_s = scratch[:, 2048:3072].bitcast(F16).rearrange("p (r s n) -> p r s n", r=2, s=2)
        h_f = scratch[:, 3072:3584]
        s_f = scratch[:, 3584:4096]
        squares = scratch[:, 0:2048].bitcast(BF16).rearrange("p (r k n) -> p r k n", r=2, k=KB)
        fly = x_ln[:, :, :].rearrange("p t n -> p (t n)")
        raw_attn = [ctx_f[:, :, :],
                    ctx_s[:, :, :, :].rearrange("p s k n -> p (s k n)").bitcast(F32)
                    .rearrange("p (k n) -> p k n", k=KB),
                    x_res[:, :, :], x_res[:, :, :]]

        vec = sb("vec", [P, VECS])
        row = sb("row", [P, 2, D])
        bo_row, ws_dp_row = row[:, 0, :], row[:, 1, :]
        ident = sb("ident", [P, P])
        hada = sb("hada", [P, P])
        amax = sb("amax", [P, MAXIMA])
        amax_all = sb("amax_all", [P, MAXIMA])
        norms = sb("norms", [P, ROOTS])
        half = sb("half", [P, ROOTS])
        ones = sb("ones", [P, 1], BF16)
        pw = sb("pw", [P, NI])
        s_attn, i_attn = sb("s_attn", [P, 4]), sb("i_attn", [P, 4])
        s_ug, i_ug = sb("s_ug", [P, 2]), sb("i_ug", [P, 2])
        coef_ug = sb("coef_ug", [P, 2, KB])
        bound = sb("bound", [P, NI])
        s_h, i_h = sb("s_h", [P, NI]), sb("i_h", [P, NI])
        gate_out = sb("gate_out", [P, NI])
        up_out = sb("up_out", [P, NI])
        coef_down = sb("coef_down", [P, NI])
        s_d, i_d = sb("s_d", [P, 1]), sb("i_d", [P, 1])
        su2 = sb("su2", [P, 1])
        stats = sb("stats", [P, TB, 6])
        mean_var = sb("mean_var", [P, TB, 2])
        var_eps, rstd = sb("var_eps", [P, TB]), sb("rstd", [P, TB])
        minus_half = sb("minus_half", [P, TB])
        ctx_max, ctx_max_all = sb("ctx_max", [P, KB + 1]), sb("ctx_max_all", [P, 1])
        s_c, i_c, o_out = sb("s_c", [P, 1]), sb("i_c", [P, 1]), sb("o_out", [P, 1])

        ring = [ctx.enter_context(nc.psum_tensor(f"ring{i}", [P, 512], F32)) for i in range(4)]
        down_ps = [ctx.enter_context(nc.psum_tensor(f"down{i}", [P, 512], F32)) for i in range(TB)]

        ident_loaded, consts_loaded = sem("ident_loaded"), sem("consts_loaded")
        attn_raw_loaded = [sem(f"attn_raw_loaded{m}") for m in range(4)]
        unit_loaded = [sem(f"unit_loaded{u}") for u in range(len(UNITS))]
        x_ln_loaded, x_res_loaded, out_stored = sem("x_ln_loaded"), sem("x_res_loaded"), sem("out_stored")
        prep_step = sem("prep_step")
        dve_step = sem("dve_step")
        halves_set, ones_set = sem("halves_set"), sem("ones_set")
        squared, normed = sem("squared"), sem("normed")
        norms_read, norms_ready = sem("norms_read"), sem("norms_ready")
        pool_passed, dve_passed = sem("pool_passed"), sem("dve_passed")
        max_ready, max_all_ready = sem("max_ready"), sem("max_all_ready")
        attn_hi, attn_split = sem("attn_hi"), sem("attn_split")
        flown = sem("flown")
        hada_done, ffn_hi, ffn_split = sem("hada_done"), sem("ffn_hi"), sem("ffn_split")
        coef_ready = sem("coef_ready")
        var_ready, rstd_ready = sem("var_ready"), sem("rstd_ready")
        xn_ready, xp_done, xt_hi, xt_ready = sem("xn_ready"), sem("xp_done"), sem("xt_hi"), sem("xt_ready")
        qkv_done = sem("qkv_done")
        k_evicted, v_evicted, q_evicted = sem("k_evicted"), sem("v_evicted"), sem("q_evicted")
        v_used, ctx_made = sem("v_used"), sem("ctx_made")
        ctx_max_ready, ctx_max_all_ready, ctx_split = sem("ctx_max_ready"), sem("ctx_max_all_ready"), sem("ctx_split")
        gate_done, up_done = sem("gate_done"), sem("up_done")
        silu_ready, up_read, h_ready, down_step = sem("silu_ready"), sem("up_read"), sem("h_ready"), sem("down_step")
        z_ready, gate_ready = sem("z_ready"), sem("gate_ready")
        o_done, o_read, out_ready = sem("o_done"), sem("o_read"), sem("out_ready")

        block = ctx.enter_context(nc.Block())

        def tokens(i):
            return x[i, :, :].rearrange("(t p) d -> p t d", p=P)

        @block.sync
        def _(sp):
            def load_x_ln(c):
                sp.dma_start(x_ln[:, :, :], tokens(c)).then_inc(x_ln_loaded, 16)

            def load_x_res(c):
                sp.dma_start(x_res[:, :, :], tokens(c)).then_inc(x_res_loaded, 16)

            def store(c):
                for t in range(TB):
                    sp.wait_ge(out_ready, 4 * c + t + 1)
                    sp.dma_start(out[c, t * P:(t + 1) * P, :], x_res[:, t, :]).then_inc(out_stored, 16)
                sp.wait_ge(out_stored, 64 * c + 64)

            def load_attn(m, w):
                sp.dma_start(raw_attn[m], w.rearrange("(k p) n -> p k n", p=P)).then_inc(attn_raw_loaded[m], 16)

            load_x_ln(0)
            sp.dma_start(ident[:, :], ident_in).then_inc(ident_loaded, 16)
            load_attn(K, wk_t)
            sp.dma_start(vec[:, :], vecs).then_inc(consts_loaded, 16)
            load_attn(V, wv_t)
            load_attn(Q, wq_t)
            sp.dma_start(hada[:, :], hada_in).then_inc(consts_loaded, 16)
            sp.dma_start(row[:, :, :], rows.partition_broadcast(P)).then_inc(consts_loaded, 16)
            for u, (b, m) in enumerate(UNITS):
                if m is None:
                    dst, src = down_raw[:, 4 * b:4 * b + 4, :], down_t[b * 512:(b + 1) * 512, :]
                else:
                    dst, src = ug_raw[:, m, b, :, :], (gate_t, up_t)[m][:, b * 512:(b + 1) * 512]
                sp.dma_start(dst, src.rearrange("(k p) n -> p k n", p=P)).then_inc(unit_loaded[u], 16)
            sp.wait_ge(attn_split, 12)
            load_attn(O, wo_t)
            sp.wait_ge(flown, 1 + UG_UNITS)
            load_x_ln(1)
            sp.wait_ge(attn_split, 16)
            load_x_res(0)
            with sp.Fori(0, CHUNKS - 2) as c:
                sp.wait_ge(xp_done, 4 * c + 8)
                load_x_ln(c + 2)
                store(c)
                load_x_res(c + 1)
            store(CHUNKS - 2)
            load_x_res(CHUNKS - 1)
            store(CHUNKS - 1)

        @block.gpsimd
        def _(pool):
            pool.memset(minus_half[:, :], -0.5).then_inc(halves_set, 1)
            pool.memset(half[:, :], 0.5).then_inc(halves_set, 1)
            pool.wait_ge(halves_set, 2)

            def rstd_of(n):
                pool.wait_ge(var_ready, n + 1)
                pool.tensor_tensor(rstd[:, :], var_eps[:, :], minus_half[:, :], ALU.pow).then_inc(rstd_ready, 1)

            def ctx_max_of(c):
                pool.wait_ge(ctx_max_ready, c + 1)
                pool.sem_inc(pool_passed, 1)
                pool.partition_all_reduce(ctx_max_all[:, :], ctx_max[:, KB:KB + 1], P, REDUCE_MAX) \
                    .then_inc(ctx_max_all_ready, 1)

            def weight_max(n, a, b):
                pool.wait_ge(max_ready, n + 1)
                pool.partition_all_reduce(amax_all[:, a:b], amax[:, a:b], P, REDUCE_MAX) \
                    .then_inc(max_all_ready, 1)

            rstd_of(0)
            for n, m in enumerate((K, V, Q)):
                weight_max(n, m, m + 1)
            weight_max(3, M_SU, M_SU + 1)
            ctx_max_of(0)
            pool.wait_ge(norms_read, 1)
            pool.tensor_tensor(norms[:, :], norms[:, :], half[:, :], ALU.pow).then_inc(norms_ready, 1)
            weight_max(4, M_GATE, M_DOWN + 1)
            weight_max(5, M_COEF, M_COEF + 1)
            weight_max(6, O, O + 1)
            rstd_of(1)
            with pool.Fori(1, CHUNKS - 1) as c:
                ctx_max_of(c)
                rstd_of(c + 1)
            ctx_max_of(CHUNKS - 1)

        @block.scalar
        def _(act):
            def split_attn(m):
                for k in range(KB):
                    act.activation(w_attn[:, m, HI, k, :], raw_attn[m][:, k, :], ACT.Copy,
                                   scale=s_attn[:, m:m + 1]).then_inc(attn_hi, 1)

            def xt_high(c):
                for k in range(KB):
                    act.wait_ge(xp_done, 4 * c + k + 1)
                    act.activation(xt[:, HI, k, :], ring[k][:, :], ACT.Copy).then_inc(xt_hi, 1)

            def square(u):
                b, m = UNITS[u]
                raw = down_raw[:, 4 * b:4 * b + 4, :] if m is None else ug_raw[:, m, b, :, :]
                act.wait_ge(unit_loaded[u], 16)
                if u >= 2:
                    act.wait_ge(normed, u - 1)
                act.activation(squares[:, u % 2, :, :], raw, ACT.Square).then_inc(squared, 1)

            def evict_qkv(c, units=()):
                units = list(units)
                for f in range(KB):
                    for j, m in enumerate((K, V, Q)):
                        n = 3 * f + j
                        bank = ring[n % 4]
                        act.wait_ge(qkv_done, 12 * c + n + 1)
                        if n and units:
                            square(units.pop(0))
                        unscale = i_attn[:, m:m + 1]
                        if m == V:
                            if not (isinstance(c, int) and c == 0 and f == 0):
                                act.wait_ge(v_used, 4 * c + f)
                            act.activation(v_sb[:, :], bank[:, :], ACT.Identity,
                                           bias=vec[:, BV + f:BV + f + 1], scale=unscale).then_inc(v_evicted, 1)
                            continue
                        e, r, b, done = (e_k, r_k, BK, k_evicted) if m == K else (e_q, r_q, BQ, q_evicted)
                        if not (isinstance(c, int) and c == 0 and f == 0):
                            act.wait_ge(ctx_made, 4 * c + f)
                        act.activation(e[:, :], bank[:, :], ACT.Exp, bias=vec[:, b + f:b + f + 1], scale=unscale)
                        act.activation(r[:, :], bank[:, :], ACT.Relu, bias=vec[:, b + f:b + f + 1],
                                       scale=unscale).then_inc(done, 1)
                for u in units:
                    square(u)

            def split_part(b, m):
                for k in range(KB):
                    act.wait_ge(hada_done, NI + (2 * b + m) * KB + k + 1)
                    act.activation(ug[:, m, b, k, HI, :], ring[k][:, :], ACT.Copy,
                                   scale=coef_ug[:, m, k:k + 1]).then_inc(ffn_hi, 1)

            def silu_gates(c):
                first = isinstance(c, int) and c == 0
                for i in range(NI):
                    act.wait_ge(gate_done, 16 * c + i + 1)
                    if not (isinstance(c, int) and c == 0 and i < 2):
                        act.wait_ge(up_read, 16 * c + i - 1)
                    act.activation(silu[:, i % 2, :], ring[(12 + 2 * i) % 4][:, :], ACT.Silu,
                                   scale=gate_out[:, i:i + 1]).then_inc(silu_ready, 1)
                    if first and i % 4 in (1, 2) and i // 4 + 1 < BLOCKS:
                        split_part(i // 4 + 1, i % 4 - 1)
                    if first and i == 12:
                        act.wait_ge(coef_ready, 6)
                        split_attn(O)

            def silu_outs(c):
                for t in range(TB):
                    act.wait_ge(z_ready, 4 * c + t + 1)
                    act.activation(gate_g[:, t % 2, :], gate_g[:, t % 2, :], ACT.Silu).then_inc(gate_ready, 1)

            act.wait_ge(coef_ready, 1)
            split_attn(K)
            xt_high(0)
            for n, m in enumerate((V, Q)):
                act.wait_ge(coef_ready, 2 + n)
                split_attn(m)
            act.wait_ge(consts_loaded, 48)
            evict_qkv(0, range(len(UNITS)))
            act.wait_ge(coef_ready, 5)
            for k in range(NI):
                act.wait_ge(hada_done, k + 1)
                act.activation(down[:, k, HI, :], down_ps[k % 4][:, :], ACT.Copy,
                               scale=coef_down[:, k:k + 1]).then_inc(ffn_hi, 1)
            split_part(0, GATE)
            split_part(0, UP)
            silu_gates(0)
            xt_high(1)
            silu_outs(0)
            with act.Fori(1, CHUNKS - 1) as c:
                evict_qkv(c)
                silu_gates(c)
                xt_high(c + 1)
                silu_outs(c)
            evict_qkv(CHUNKS - 1)
            silu_gates(CHUNKS - 1)
            silu_outs(CHUNKS - 1)

        @block.vector
        def _(dve):
            class Chain:

                def __init__(self, counter, base):
                    self.counter, self.base, self.n = counter, base, 0

                def after(self, ins):
                    self.n += 1
                    ins.then_inc(self.counter, 1)
                    dve.wait_ge(self.counter, self.base + self.n)

            prep = Chain(prep_step, 0)

            def pow2(chain, src, factor, scale, inverse):
                t = pw[:, 0:src.free_size()]
                chain.after(dve.tensor_scalar(t, src, factor, None, ALU.mult))
                chain.after(dve.tensor_scalar(t.bitcast(I32), t.bitcast(I32), EXPONENT, None, ALU.bitwise_and))
                chain.after(dve.tensor_scalar(inverse.bitcast(I32), t.bitcast(I32), float(TINY << 23),
                                              -float(TOP << 23), ALU.max, ALU.add))
                chain.after(dve.tensor_scalar(scale.bitcast(I32), inverse.bitcast(I32), -1.0,
                                              float(254 << 23), ALU.mult, ALU.add))

            def absmax(dst, src):
                return dve.tensor_reduce(dst, src, AX_X, ALU.max, apply_absolute_value=True)

            def flat(ap):
                return ap.rearrange("p k n -> p (k n)")

            def ln_stats(c, chain):
                dve.wait_ge(x_ln_loaded, 16 * c + 16)
                for t in range(TB):
                    last = dve.bn_stats(stats[:, t, :], x_ln[:, t, :])
                chain.after(last)
                dve.sem_inc(dve_passed, 1)
                for t in range(TB):
                    last = dve.bn_aggr(mean_var[:, t, :], stats[:, t, :])
                chain.after(last)
                dve.tensor_scalar(var_eps[:, :], mean_var[:, :, 1], EPS, None, ALU.add).then_inc(var_ready, 1)

            def ln_scale(c, chain):
                dve.wait_ge(rstd_ready, c + 1)
                chain.after(dve.tensor_scalar(rstd[:, :], rstd[:, :], X_SCALE, None, ALU.mult))

            def normalise(t):
                dve.tensor_scalar(x_ln[:, t, :], x_ln[:, t, :], mean_var[:, t, 0:1], rstd[:, t:t + 1],
                                  ALU.subtract, ALU.mult).then_inc(xn_ready, 1)

            def xt_low(c):
                for k in range(KB):
                    dve.wait_ge(xt_hi, 4 * c + k + 1)
                    dve.tensor_tensor(xt[:, LO, k, :], ring[k][:, :], xt[:, HI, k, :], ALU.subtract) \
                        .then_inc(xt_ready, 1)

            def attention(c, chain):
                for f in range(KB):
                    dve.wait_ge(k_evicted, 4 * c + f + 1)
                    chain.after(dve.scalar_tensor_tensor(e_k[:, :], e_k[:, :], 1.0, r_k[:, :], ALU.min, ALU.add))
                    dve.wait_ge(v_evicted, 4 * c + f + 1)
                    dve.tensor_tensor(e_k[:, :], e_k[:, :], v_sb[:, :], ALU.mult).then_inc(v_used, 1)
                    dve.wait_ge(v_used, 4 * c + f + 1)
                    dve.tensor_tensor_scan(r_k[:, :], e_k[:, :], e_k[:, :], 0.0, ALU.add, ALU.bypass)
                    dve.wait_ge(q_evicted, 4 * c + f + 1)
                    chain.after(dve.scalar_tensor_tensor(e_q[:, :], e_q[:, :], 1.0, r_q[:, :], ALU.min, ALU.add))
                    dve.tensor_tensor(ctx_f[:, f, :], e_q[:, :], r_k[:, :], ALU.mult).then_inc(ctx_made, 1)
                    dve.wait_ge(ctx_made, 4 * c + f + 1)
                    last = absmax(ctx_max[:, f:f + 1], ctx_f[:, f, :])
                chain.after(last)
                dve.tensor_reduce(ctx_max[:, KB:KB + 1], ctx_max[:, 0:KB], AX_X, ALU.max).then_inc(ctx_max_ready, 1)

            def ctx_scale(c, chain):
                dve.wait_ge(ctx_max_all_ready, c + 1)
                pow2(chain, ctx_max_all[:, 0:1], 1.0, s_c[:, :], i_c[:, :])
                if not (isinstance(c, int) and c == 0):
                    take_back_o(chain)

            def take_back_o(chain):
                chain.after(dve.tensor_scalar(o_out[:, :], i_c[:, :], i_attn[:, O:O + 1], HEAD_DIM ** -0.5,
                                              ALU.mult, ALU.mult))

            def split_ctx(f, chain):
                chain.after(dve.tensor_scalar(ctx_s[:, HI, f, :], ctx_f[:, f, :], s_c[:, 0:1], None, ALU.mult))
                dve.scalar_tensor_tensor(ctx_s[:, LO, f, :], ctx_f[:, f, :], s_c[:, 0:1], ctx_s[:, HI, f, :],
                                         ALU.mult, ALU.subtract).then_inc(ctx_split, 1)

            def hidden(c, i, chain):
                dve.wait_ge(silu_ready, 16 * c + i + 1)
                dve.wait_ge(up_done, 16 * c + i + 1)
                if not (isinstance(c, int) and c == 0 and i == 0):
                    dve.wait_ge(h_ready, 16 * c + i)
                dve.scalar_tensor_tensor(h_f, ring[(13 + 2 * i) % 4][:, :], up_out[:, i:i + 1], silu[:, i % 2, :],
                                         ALU.mult, ALU.mult).then_inc(up_read, 1)
                dve.wait_ge(up_read, 16 * c + i + 1)
                if not (isinstance(c, int) and c == 0 and i < 2):
                    dve.wait_ge(down_step, 16 * c + i - 1)
                chain.after(dve.tensor_copy(h_s[:, i % 2, HI, :], h_f))
                dve.tensor_tensor(h_s[:, i % 2, LO, :], h_f, h_s[:, i % 2, HI, :], ALU.subtract).then_inc(h_ready, 1)

            def gate_argument(c, t):
                if t == 0:
                    dve.wait_ge(down_step, 16 * c + 16)
                dve.scalar_tensor_tensor(gate_g[:, t % 2, :], down_ps[t][:, :], i_d[:, 0:1], ws_dp_row,
                                         ALU.mult, ALU.mult).then_inc(z_ready, 1)

            def outputs(c, chain):
                gate_argument(c, 0)
                gate_argument(c, 1)
                for t in range(TB):
                    dve.wait_ge(o_done, 4 * c + t + 1)
                    if not (isinstance(c, int) and c == 0 and t == 0):
                        dve.wait_ge(out_ready, 4 * c + t)
                    dve.scalar_tensor_tensor(s_f, ring[t][:, :], o_out[:, 0:1], bo_row, ALU.mult, ALU.add) \
                        .then_inc(o_read, 1)
                    dve.wait_ge(o_read, 4 * c + t + 1)
                    dve.wait_ge(gate_ready, 4 * c + t + 1)
                    chain.after(dve.tensor_tensor(s_f, s_f, gate_g[:, t % 2, :], ALU.mult))
                    if t + 2 < TB:
                        gate_argument(c, t + 2)
                    if t == 0:
                        dve.wait_ge(x_res_loaded, 16 * c + 16)
                    dve.tensor_tensor(x_res[:, t, :], x_res[:, t, :], s_f, ALU.add).then_inc(out_ready, 1)

            def feed_forward(c, chain, last):
                first = isinstance(c, int) and c == 0
                at = 10 if first else 6
                for i in range(NI):
                    hidden(c, i, chain)
                    if first and i % 4 == 0 and i // 4 + 1 < BLOCKS:
                        fly_block(i // 4 + 1)
                    if first and i % 4 in (1, 2) and i // 4 + 1 < BLOCKS:
                        split_part(i // 4 + 1, i % 4 - 1)
                    if first and i == 11:
                        prepare_o()
                    if first and i == 12:
                        split_attn(3, O)
                    if i == 1:
                        ctx_scale(c, chain)
                    if 2 <= i < 2 + KB:
                        split_ctx(i - 2, chain)
                    if not last and i == at:
                        ln_stats(c + 1, chain)
                    if not last and i == at + 1:
                        ln_scale(c + 1, chain)
                    if not last and at + 2 <= i < at + 2 + TB:
                        normalise(i - at - 2)
                if not last:
                    xt_low(c + 1)
                outputs(c, chain)

            def weight_scale(n, m):
                dve.wait_ge(max_all_ready, n + 1)
                pow2(prep, amax_all[:, m:m + 1], 1.0, s_attn[:, m:m + 1], i_attn[:, m:m + 1])
                dve.tensor_scalar(i_attn[:, m:m + 1], i_attn[:, m:m + 1], 1.0 if m == O else 1.0 / X_SCALE,
                                  None, ALU.mult).then_inc(coef_ready, 1)

            def weight_max(m):
                dve.wait_ge(attn_raw_loaded[m], 16)
                absmax(amax[:, m:m + 1], flat(raw_attn[m])).then_inc(max_ready, 1)

            def split_attn(n, m):
                for k in range(KB):
                    dve.wait_ge(attn_hi, 4 * n + k + 1)
                    dve.scalar_tensor_tensor(w_attn[:, m, LO, k, :], raw_attn[m][:, k, :], s_attn[:, m:m + 1],
                                             w_attn[:, m, HI, k, :], ALU.mult, ALU.subtract).then_inc(attn_split, 1)

            def prepare_o():
                weight_max(O)
                weight_scale(6, O)
                dve.wait_ge(coef_ready, 6)
                take_back_o(prep)

            def butterfly(src, dst, half):
                a = src.rearrange("p (a two b) n -> p a two b n", two=2, b=half)
                d = dst.rearrange("p (a two b) n -> p a two b n", two=2, b=half)
                dve.tensor_tensor(d[:, :, 0], a[:, :, 0], a[:, :, 1], ALU.add)
                return dve.tensor_tensor(d[:, :, 1], a[:, :, 0], a[:, :, 1], ALU.subtract)

            fly_ug = fly.rearrange("p (k n) -> p k n", k=KB)
            fly_down = fly.rearrange("p (k n) -> p k n", k=NI)

            def fly_columns(g):
                cols = down_raw[:, :, g * P:(g + 1) * P]
                for src, dst, half in ((cols, fly_down, 1), (fly_down, cols, 2), (cols, fly_down, 4)):
                    prep.after(butterfly(src, dst, half))
                last = butterfly(fly_down, cols, 8)
                if g < NI // KB - 1:
                    prep.after(last)
                else:
                    last.then_inc(flown, 1)

            def fly_block(b):
                for m in (GATE, UP):
                    dve.wait_ge(flown, 1 + 2 * b + m)
                    prep.after(butterfly(ug_raw[:, m, b, :, :], fly_ug, 1))
                    butterfly(fly_ug, ug_raw[:, m, b, :, :], 2).then_inc(flown, 1)

            def split_part(b, m):
                for k in range(KB):
                    n = NI + (2 * b + m) * KB + k
                    dve.wait_ge(ffn_hi, n + 1)
                    dve.scalar_tensor_tensor(ug[:, m, b, k, LO, :], ring[k][:, :], coef_ug[:, m, k:k + 1],
                                             ug[:, m, b, k, HI, :], ALU.mult, ALU.subtract).then_inc(ffn_split, 1)

            dve.memset(ones[:, :], 1.0).then_inc(ones_set, 1)
            ln_stats(0, prep)
            ln_scale(0, prep)
            for t in range(TB):
                normalise(t)
            weight_max(K)
            weight_scale(0, K)
            weight_max(V)
            xt_low(0)
            split_attn(0, K)
            weight_scale(1, V)
            weight_max(Q)
            split_attn(1, V)
            weight_scale(2, Q)
            split_attn(2, Q)
            dve.wait_ge(consts_loaded, 48)
            absmax(amax[:, M_SU:M_SU + 1], vec[:, SU_UG:SU_UG + KB]).then_inc(max_ready, 1)

            chain = Chain(dve_step, 0)
            attention(0, chain)
            dve.wait_ge(normed, len(UNITS))
            n_ps = down_ps[0]
            prep.after(dve.tensor_copy(norms[:, 0:2 * NI], n_ps[:, 0:2 * NI]))
            prep.after(dve.tensor_reduce(norms[:, 2 * NI:ROOTS],
                                         n_ps[:, 2 * NI:2 * NI + 16].rearrange("p (g n) -> p n g", g=NI // KB),
                                         AX_X, ALU.add))
            dve.tensor_scalar(norms[:, :], norms[:, :], MARGIN, TINY_SQUARE, ALU.mult, ALU.max).then_inc(norms_read, 1)
            fly_columns(0)
            dve.wait_ge(norms_ready, 1)
            prep.after(dve.tensor_reduce(amax[:, M_GATE:M_UP + 1], norms[:, 0:2 * NI].rearrange("p (m i) -> p m i", m=2),
                                         AX_X, ALU.max))
            dve.tensor_reduce(amax[:, M_DOWN:M_DOWN + 1], norms[:, 2 * NI:ROOTS], AX_X, ALU.max).then_inc(max_ready, 1)
            dve.wait_ge(max_all_ready, 4)
            prep.after(dve.tensor_tensor(su2[:, :], amax_all[:, M_SU:M_SU + 1], amax_all[:, M_SU:M_SU + 1], ALU.mult))
            prep.after(dve.tensor_tensor(bound[:, :], vec[:, WS_GATE:WS_GATE + NI], vec[:, WS_UP:WS_UP + NI], ALU.mult))
            prep.after(dve.tensor_scalar(bound[:, :], bound[:, :], su2[:, 0:1], float(D), ALU.mult, ALU.mult))
            prep.after(dve.tensor_tensor(bound[:, :], bound[:, :], norms[:, 0:NI], ALU.mult))
            prep.after(dve.tensor_tensor(bound[:, :], bound[:, :], norms[:, NI:2 * NI], ALU.mult))
            pow2(prep, bound[:, :], 1.0, s_h[:, :], i_h[:, :])
            prep.after(dve.tensor_tensor(coef_down[:, :], vec[:, SU_DP:SU_DP + NI], i_h[:, :], ALU.mult))
            fly_columns(1)
            dve.wait_ge(max_all_ready, 5)
            absmax(amax[:, M_COEF:M_COEF + 1], coef_down[:, :]).then_inc(max_ready, 1)
            prep.after(dve.tensor_scalar(pw[:, 2:4], amax_all[:, M_GATE:M_UP + 1], amax_all[:, M_SU:M_SU + 1],
                                         None, ALU.mult))
            pow2(prep, pw[:, 2:4], D ** 0.5, s_ug[:, :], i_ug[:, :])
            for m, w in ((GATE, WS_GATE), (UP, WS_UP)):
                prep.after(dve.tensor_scalar(coef_ug[:, m, :], vec[:, SU_UG:SU_UG + KB], s_ug[:, m:m + 1],
                                             None, ALU.mult))
                dst = gate_out if m == GATE else up_out
                prep.after(dve.tensor_scalar(dst[:, :], vec[:, w:w + NI], i_ug[:, m:m + 1],
                                             D ** -0.5 / X_SCALE, ALU.mult, ALU.mult))
            dve.tensor_tensor(up_out[:, :], up_out[:, :], s_h[:, :], ALU.mult).then_inc(coef_ready, 1)
            fly_columns(2)
            dve.wait_ge(max_all_ready, 6)
            prep.after(dve.tensor_tensor(pw[:, 4:5], amax_all[:, M_COEF:M_COEF + 1],
                                         amax_all[:, M_DOWN:M_DOWN + 1], ALU.mult))
            pow2(prep, pw[:, 4:5], F ** 0.5, s_d[:, :], i_d[:, :])
            prep.after(dve.tensor_scalar(coef_down[:, :], coef_down[:, :], s_d[:, 0:1], None, ALU.mult))
            dve.tensor_scalar(i_d[:, :], i_d[:, :], F ** -0.5, None, ALU.mult).then_inc(coef_ready, 1)
            fly_columns(3)
            fly_block(0)
            for k in range(NI):
                dve.wait_ge(ffn_hi, k + 1)
                dve.scalar_tensor_tensor(down[:, k, LO, :], down_ps[k % 4][:, :], coef_down[:, k:k + 1],
                                         down[:, k, HI, :], ALU.mult, ALU.subtract).then_inc(ffn_split, 1)
            split_part(0, GATE)
            split_part(0, UP)

            feed_forward(0, chain, False)
            before = chain.n
            steps = before + 1
            with dve.Fori(1, CHUNKS - 1) as c:
                chain = Chain(dve_step, c * steps - (steps - before))
                attention(c, chain)
                feed_forward(c, chain, False)
                assert chain.n == steps
            chain = Chain(dve_step, (CHUNKS - 1) * steps - (steps - before))
            attention(CHUNKS - 1, chain)
            feed_forward(CHUNKS - 1, chain, True)

        @block.tensor
        def _(pe):
            def product(bank, pairs):
                for n, (lhs, rhs) in enumerate(pairs):
                    mm = pe.matmul(bank[:, :], lhs, rhs, start=(n == 0), stop=(n == len(pairs) - 1))
                return mm

            def transposes(c):
                pe.wait_ge(xn_ready, 4 * c + 4)
                for k in range(KB):
                    if not (isinstance(c, int) and c == 0):
                        if k % 2 == 0:
                            pe.wait_ge(silu_ready, 16 * c - 1 + k // 2)
                        else:
                            pe.wait_ge(up_read, 16 * c - 1 + k // 2)
                    for t in range(TB):
                        mm = pe.transpose(ring[k][:, t * P:(t + 1) * P], x_ln[:, t, k * P:(k + 1) * P], ident[:, :])
                    mm.then_inc(xp_done, 1)

            def norm(u):
                b, m = UNITS[u]
                at = 2 * NI + 4 * b if m is None else m * NI + 4 * b
                pe.wait_ge(squared, u + 1)
                for n in range(4):
                    for k in range(KB):
                        mm = pe.matmul(down_ps[0][:, at + n:at + n + 1], squares[:, u % 2, k, n * P:(n + 1) * P],
                                       ones[:, :], start=(k == 0), stop=(k == KB - 1))
                mm.then_inc(normed, 1)

            def qkv(c, units=()):
                units = list(units)
                pe.wait_ge(xt_ready, 4 * c + 4)
                for f in range(KB):
                    for j, m in enumerate((K, V, Q)):
                        n = 3 * f + j
                        if n < 4:
                            if not (isinstance(c, int) and c == 0):
                                pe.wait_ge(o_read, 4 * c - 4 + n + 1)
                        else:
                            before = (n - 4) // 3
                            pe.wait_ge((k_evicted, v_evicted, q_evicted)[(n - 4) % 3], 4 * c + before + 1)
                        if isinstance(c, int) and c == 0 and f == 0:
                            pe.wait_ge(attn_split, 4 * j + 4)
                        cols = slice(f * P, (f + 1) * P)
                        pairs = []
                        for k in range(KB):
                            w_hi, w_lo = w_attn[:, m, HI, k, cols], w_attn[:, m, LO, k, cols]
                            pairs += [(w_hi, xt[:, HI, k, :]), (w_hi, xt[:, LO, k, :]), (w_lo, xt[:, HI, k, :])]
                        product(ring[n % 4], pairs).then_inc(qkv_done, 1)
                        if n >= 2 and units:
                            norm(units.pop(0))
                for u in units:
                    norm(u)

            def gate_or_up(c, i, m):
                n = 2 * i + m
                first = isinstance(c, int) and c == 0
                b = i // 4
                if first and i < 2:
                    pe.wait_ge(ffn_split, NI + 2 * KB)
                elif first and i % 4 == 2 and b + 1 < BLOCKS:
                    pe.wait_ge(ffn_split, NI + 2 * (b + 1) * KB + m + 1)
                elif first and i % 4 == 3 and b + 1 < BLOCKS:
                    pe.wait_ge(ffn_split, NI + (2 * (b + 1) + 1) * KB + 2 + m + 1)
                elif first and i % 4 == 0:
                    pe.wait_ge(ffn_split, NI + (2 * b + 1) * KB + (KB if m == UP else 1))
                elif n < 4:
                    pe.wait_ge((k_evicted, v_evicted, q_evicted)[(8 + n) % 3], 4 * c + (8 + n) // 3 + 1)
                else:
                    pe.wait_ge(silu_ready if m == GATE else up_read, 16 * c + i - 1)
                cols = slice(i % 4 * P, (i % 4 + 1) * P)
                pairs = []
                for k in range(KB):
                    w_hi, w_lo = ug[:, m, i // 4, k, HI, cols], ug[:, m, i // 4, k, LO, cols]
                    pairs += [(w_hi, xt[:, HI, k, :]), (w_hi, xt[:, LO, k, :]), (w_lo, xt[:, HI, k, :])]
                product(ring[(12 + n) % 4], pairs).then_inc(gate_done if m == GATE else up_done, 1)

            def down_product(c, i):
                if i == 0:
                    if isinstance(c, int) and c == 0:
                        pe.wait_ge(ffn_split, NI)
                    else:
                        pe.wait_ge(gate_ready, 4 * c)
                pe.wait_ge(h_ready, 16 * c + i + 1)
                for t in range(TB):
                    cols = slice(t * P, (t + 1) * P)
                    pairs = ((h_s[:, i % 2, HI, cols], down[:, i, HI, :]), (h_s[:, i % 2, HI, cols], down[:, i, LO, :]),
                             (h_s[:, i % 2, LO, cols], down[:, i, HI, :]))
                    for n, (lhs, rhs) in enumerate(pairs):
                        mm = pe.matmul(down_ps[t][:, :], lhs, rhs, start=(i == 0 and n == 0),
                                       stop=(i == NI - 1 and n == 2))
                mm.then_inc(down_step, 1)

            def out_product(c, last):
                pe.wait_ge(ctx_split, 4 * c + 4)
                if isinstance(c, int) and c == 0:
                    pe.wait_ge(attn_split, 16)
                for t in range(TB):
                    if not last:
                        pe.wait_ge(xt_ready, 4 * c + 4 + t + 1)
                    elif t % 2 == 0:
                        pe.wait_ge(silu_ready, 16 * c + 15 + t // 2)
                    else:
                        pe.wait_ge(up_read, 16 * c + 15 + t // 2)
                    cols = slice(t * P, (t + 1) * P)
                    pairs = []
                    for f in range(KB):
                        c_hi, c_lo = ctx_s[:, HI, f, cols], ctx_s[:, LO, f, cols]
                        pairs += [(c_hi, w_attn[:, O, HI, f, :]), (c_hi, w_attn[:, O, LO, f, :]),
                                  (c_lo, w_attn[:, O, HI, f, :])]
                    product(ring[t], pairs).then_inc(o_done, 1)

            def hadamard(b, m):
                pe.wait_ge(flown, 2 + 2 * b + m)
                for k in range(KB):
                    if b == 0 and m == GATE:
                        pe.wait_ge(q_evicted, KB)
                    elif b == 0 or (m == UP and k >= 2):
                        pe.wait_ge(ffn_split, NI + 2 * b * KB + k + 1)
                    else:
                        pe.wait_ge((silu_ready, up_read)[k % 2], 4 * (b - 1) + (2 if m == UP else k // 2) + 1)
                    pe.matmul(ring[k][:, :], hada[:, :], ug_raw[:, m, b, k, :], start=True, stop=True) \
                        .then_inc(hada_done, 1)

            def feed_forward(c, last):
                for i in range(NI):
                    gate_or_up(c, i, GATE)
                    gate_or_up(c, i, UP)
                    if i >= 1:
                        down_product(c, i - 1)
                    if isinstance(c, int) and c == 0 and i % 4 in (1, 2) and i // 4 + 1 < BLOCKS:
                        hadamard(i // 4 + 1, i % 4 - 1)
                if not last:
                    transposes(c + 1)
                down_product(c, NI - 1)
                out_product(c, last)

            pe.wait_ge(ident_loaded, 16)
            transposes(0)
            pe.wait_ge(ones_set, 1)
            qkv(0, range(len(UNITS)))
            pe.wait_ge(consts_loaded, 48)
            pe.wait_ge(flown, 1)
            pe.wait_ge(norms_read, 1)
            for k in range(NI):
                if k >= 4:
                    pe.wait_ge(ffn_split, k - 3)
                pe.matmul(down_ps[k % 4][:, :], hada[:, :], down_raw[:, k, :], start=True, stop=True) \
                    .then_inc(hada_done, 1)
            hadamard(0, GATE)
            hadamard(0, UP)
            feed_forward(0, False)
            with pe.Fori(1, CHUNKS - 1) as c:
                qkv(c)
                feed_forward(c, False)
            qkv(CHUNKS - 1)
            feed_forward(CHUNKS - 1, True)


def kernel(**inputs):
    import numpy as np
    import concourse.bacc as bacc
    from concourse.bass_utils import run_bass_kernel_spmd

    def part(name):
        return np.asarray(inputs[name])

    def by_partition(v):
        return np.asarray(v).reshape(-1, P).T

    hadamard = np.ones((1, 1), np.float32)
    while hadamard.shape[0] < P:
        hadamard = np.block([[hadamard, hadamard], [hadamard, -hadamard]])
    ws_ug = part("L0_ffn_Wscale_ug")
    arrays = {
        "x": part("L0_attn_x"),
        "wk_t": part("L0_attn_Wk").T, "wv_t": part("L0_attn_Wv").T, "wq_t": part("L0_attn_Wq").T,
        "wo_t": part("L0_attn_Wo").T,
        "gate_t": part("L0_ffn_W_gate").T, "up_t": part("L0_ffn_W_up").T, "down_t": part("L0_ffn_W_down").T,
        "vecs": np.concatenate([by_partition(v) for v in (
            part("L0_attn_bk"), part("L0_attn_bv"), part("L0_attn_bq"), part("L0_ffn_SU_ug"),
            part("L0_ffn_SU_dp"), ws_ug[F:], ws_ug[:F])], axis=1),
        "rows": np.stack([part("L0_attn_bo"), part("L0_ffn_Wscale_dp")]),
        "ident": np.eye(P, dtype=np.float32),
        "hadamard": hadamard,
    }
    arrays = {f"in_{k}": np.ascontiguousarray(v) for k, v in arrays.items()}
    nc = bacc.Bacc("TRN2", target_bir_lowering=False, num_devices=1)
    args = [nc.dram_tensor(k, v.shape, mybir.dt.from_np(v.dtype), kind="ExternalInput").ap()
            for k, v in arrays.items()]
    args.append(nc.dram_tensor("out", (CHUNKS, T, D), F32, kind="ExternalOutput").ap())
    build(nc, *args)
    r = run_bass_kernel_spmd(nc, [arrays], core_ids=[0])
    return r.results[0]["out"]
```

```python
from contextlib import ExitStack

import concourse.bass as bass
from concourse import mybir

F32 = mybir.dt.float32
F16 = mybir.dt.float16
BF16 = mybir.dt.bfloat16
I32 = mybir.dt.int32
ALU = mybir.AluOpType
ACT = mybir.ActivationFunctionType
AX_X = mybir.AxisListType.X
REDUCE_MAX = bass.bass_isa.ReduceOp.max

P = 128
CHUNKS, T, D = 8, 512, 512
F = 2048
HEAD_DIM = D // 16
KB = D // P
TB = T // P
NI = F // P
BLOCKS = F // 512
EPS = 1e-5

X_SCALE = 1024.0
TOP = 14
TINY = 27
TINY_ROOT = 77
TINY_SQUARE = 2.0 ** -100
EXPONENT = 0x7F800000

BK, BV, BQ, SU_UG, SU_DP, WS_GATE, WS_UP = 0, 4, 8, 12, 16, 32, 48
VECS = 64
K, V, Q, O = range(4)
M_SU, M_GATE, M_UP, M_DOWN, M_COEF = range(4, 9)
MAXIMA = 9
GATE, UP = 0, 1
GROUPS = NI // KB
UNITS = [(0, GATE), (0, UP)] + [(g, None) for g in range(GROUPS)] \
    + [(b, m) for b in range(1, BLOCKS) for m in (GATE, UP)]
ROOTS = 2 * NI + KB
MARGIN = 1.02
HI, LO = 0, 1


def build(nc, x, wk_t, wv_t, wq_t, wo_t, gate_t, up_t, down_t, vecs, rows, ident_in, hada_in, out):
    with ExitStack() as ctx:
        def sb(name, shape, dt=F32):
            return ctx.enter_context(nc.sbuf_tensor(name, shape, dt))

        def sem(name):
            return ctx.enter_context(nc.semaphore(name))

        w_attn = sb("w_attn", [P, 4, 2, KB, D], F16)
        w_ug = sb("w_ug", [P, 2 * BLOCKS * KB * 512])
        w_down = sb("w_down", [P, NI * D])
        ug_raw = w_ug[:, :].rearrange("p (m b k n) -> p m b k n", m=2, b=BLOCKS, k=KB)
        ug = w_ug[:, :].bitcast(F16).rearrange("p (m b k s n) -> p m b k s n", m=2, b=BLOCKS, k=KB, s=2)
        down_raw = w_down[:, :].rearrange("p (k n) -> p k n", k=NI)
        down = w_down[:, :].bitcast(F16).rearrange("p (k s n) -> p k s n", k=NI, s=2)

        x_ln = sb("x_ln", [P, TB, D])
        x_res = sb("x_res", [P, TB, D])
        xt = sb("xt", [P, 2, KB, T], F16)
        e_k, r_k = sb("e_k", [P, T]), sb("r_k", [P, T])
        e_q, r_q = sb("e_q", [P, T]), sb("r_q", [P, T])
        v_sb = sb("v_sb", [P, T])
        ctx_f = sb("ctx_f", [P, KB, T])
        ctx_s = sb("ctx_s", [P, 2, KB, T], F16)
        scratch = sb("scratch", [P, 4096])
        silu = scratch[:, 0:1024].rearrange("p (r n) -> p r n", r=2)
        gate_g = scratch[:, 1024:2048].rearrange("p (r n) -> p r n", r=2)
        h_s = scratch[:, 2048:3072].bitcast(F16).rearrange("p (r s n) -> p r s n", r=2, s=2)
        h_f = scratch[:, 3072:3584]
        s_f = scratch[:, 3584:4096]
        squares = scratch[:, 0:2048].bitcast(BF16).rearrange("p (r k n) -> p r k n", r=2, k=KB)
        unkept = scratch[:, 2048:3072].bitcast(BF16)
        unkept_o = ctx_s[:, 0, :, :].rearrange("p k n -> p (k n)").bitcast(BF16)
        fly = x_ln[:, :, :].rearrange("p t n -> p (t n)")
        raw_attn = [ctx_f[:, :, :],
                    ctx_s[:, :, :, :].rearrange("p s k n -> p (s k n)").bitcast(F32)
                    .rearrange("p (k n) -> p k n", k=KB),
                    x_res[:, :, :], x_res[:, :, :]]

        vec = sb("vec", [P, VECS])
        row = sb("row", [P, 2, D])
        bo_row, ws_dp_row = row[:, 0, :], row[:, 1, :]
        ident = sb("ident", [P, P])
        hada = sb("hada", [P, P])
        amax = sb("amax", [P, MAXIMA])
        amax_all = sb("amax_all", [P, MAXIMA])
        norms = sb("norms", [P, ROOTS])
        half = sb("half", [P, ROOTS])
        ones = sb("ones", [P, 1], BF16)
        pw = sb("pw", [P, NI])
        s_attn, i_attn = sb("s_attn", [P, 4]), sb("i_attn", [P, 4])
        s_ug, i_ug = sb("s_ug", [P, 2]), sb("i_ug", [P, 2])
        coef_ug = sb("coef_ug", [P, 2, KB])
        bound = sb("bound", [P, NI])
        s_h, i_h = sb("s_h", [P, NI]), sb("i_h", [P, NI])
        gate_out = sb("gate_out", [P, NI])
        up_out = sb("up_out", [P, NI])
        coef_down = sb("coef_down", [P, NI])
        s_d, i_d = sb("s_d", [P, 1]), sb("i_d", [P, 1])
        su2 = sb("su2", [P, 1])
        stats = sb("stats", [P, TB, 6])
        mean_var = sb("mean_var", [P, TB, 2])
        var_eps, rstd = sb("var_eps", [P, TB]), sb("rstd", [P, TB])
        minus_half = sb("minus_half", [P, TB])
        ctx_max, ctx_max_all = sb("ctx_max", [P, KB + 1]), sb("ctx_max_all", [P, 1])
        s_c, i_c, o_out = sb("s_c", [P, 1]), sb("i_c", [P, 1]), sb("o_out", [P, 1])

        ring = [ctx.enter_context(nc.psum_tensor(f"ring{i}", [P, 512], F32)) for i in range(4)]
        down_ps = [ctx.enter_context(nc.psum_tensor(f"down{i}", [P, 512], F32)) for i in range(TB)]

        ident_loaded, consts_loaded = sem("ident_loaded"), sem("consts_loaded")
        attn_raw_loaded = [sem(f"attn_raw_loaded{m}") for m in range(4)]
        unit_loaded = [sem(f"unit_loaded{u}") for u in range(len(UNITS))]
        x_ln_loaded, x_res_loaded, out_stored = sem("x_ln_loaded"), sem("x_res_loaded"), sem("out_stored")
        prep_step = sem("prep_step")
        dve_step = sem("dve_step")
        halves_set, ones_set = sem("halves_set"), sem("ones_set")
        attn_squared = sem("attn_squared")
        squared, normed = sem("squared"), sem("normed")
        norms_read, norms_ready = sem("norms_read"), sem("norms_ready")
        pool_passed, dve_passed = sem("pool_passed"), sem("dve_passed")
        max_ready, max_all_ready = sem("max_ready"), sem("max_all_ready")
        attn_bounded, pool_step = sem("attn_bounded"), sem("pool_step")
        attn_hi, attn_split = sem("attn_hi"), sem("attn_split")
        flown = sem("flown")
        hada_done, ffn_hi, ffn_split = sem("hada_done"), sem("ffn_hi"), sem("ffn_split")
        coef_ready = sem("coef_ready")
        var_ready, rstd_ready = sem("var_ready"), sem("rstd_ready")
        xn_ready, xp_done, xt_hi, xt_ready = sem("xn_ready"), sem("xp_done"), sem("xt_hi"), sem("xt_ready")
        qkv_done = sem("qkv_done")
        k_evicted, v_evicted, q_evicted = sem("k_evicted"), sem("v_evicted"), sem("q_evicted")
        v_used, ctx_made = sem("v_used"), sem("ctx_made")
        ctx_max_ready, ctx_max_all_ready, ctx_split = sem("ctx_max_ready"), sem("ctx_max_all_ready"), sem("ctx_split")
        gate_done, up_done = sem("gate_done"), sem("up_done")
        silu_ready, up_read, h_ready, down_step = sem("silu_ready"), sem("up_read"), sem("h_ready"), sem("down_step")
        z_ready, gate_ready = sem("z_ready"), sem("gate_ready")
        o_done, o_read, out_ready = sem("o_done"), sem("o_read"), sem("out_ready")

        def flat_attn(m):
            return raw_attn[m].rearrange("p k n -> p (k n)")

        block = ctx.enter_context(nc.Block())

        def part_at(b, m):
            return (2 * b + m) * KB + (NI if b else 0)

        def tokens(i):
            return x[i, :, :].rearrange("(t p) d -> p t d", p=P)

        @block.sync
        def _(sp):
            def load_x_ln(c):
                sp.dma_start(x_ln[:, :, :], tokens(c)).then_inc(x_ln_loaded, 16)

            def load_x_res(c):
                sp.dma_start(x_res[:, :, :], tokens(c)).then_inc(x_res_loaded, 16)

            def store(c):
                for t in range(TB):
                    sp.wait_ge(out_ready, 4 * c + t + 1)
                    sp.dma_start(out[c, t * P:(t + 1) * P, :], x_res[:, t, :]).then_inc(out_stored, 16)
                sp.wait_ge(out_stored, 64 * c + 64)

            def load_attn(m, w):
                sp.dma_start(raw_attn[m], w.rearrange("(k p) n -> p k n", p=P)).then_inc(attn_raw_loaded[m], 16)

            load_x_ln(0)
            sp.dma_start(ident[:, :], ident_in).then_inc(ident_loaded, 16)
            load_attn(K, wk_t)
            sp.dma_start(vec[:, :], vecs).then_inc(consts_loaded, 16)
            load_attn(V, wv_t)
            load_attn(Q, wq_t)
            sp.dma_start(hada[:, :], hada_in).then_inc(consts_loaded, 16)
            sp.dma_start(row[:, :, :], rows.partition_broadcast(P)).then_inc(consts_loaded, 16)
            for u, (b, m) in enumerate(UNITS):
                if m is None:
                    dst, src = down_raw[:, 4 * b:4 * b + 4, :], down_t[b * 512:(b + 1) * 512, :]
                else:
                    dst, src = ug_raw[:, m, b, :, :], (gate_t, up_t)[m][:, b * 512:(b + 1) * 512]
                sp.dma_start(dst, src.rearrange("(k p) n -> p k n", p=P)).then_inc(unit_loaded[u], 16)
            sp.wait_ge(attn_split, 12)
            load_attn(O, wo_t)
            sp.wait_ge(flown, len(UNITS))
            load_x_ln(1)
            sp.wait_ge(attn_split, 16)
            load_x_res(0)
            with sp.Fori(0, CHUNKS - 2) as c:
                sp.wait_ge(xp_done, 4 * c + 8)
                load_x_ln(c + 2)
                store(c)
                load_x_res(c + 1)
            store(CHUNKS - 2)
            load_x_res(CHUNKS - 1)
            store(CHUNKS - 1)

        @block.gpsimd
        def _(pool):
            pool.memset(minus_half[:, :], -0.5).then_inc(halves_set, 1)
            pool.memset(half[:, :], 0.5).then_inc(halves_set, 1)
            pool.wait_ge(halves_set, 2)

            def rstd_of(n):
                pool.wait_ge(var_ready, n + 1)
                pool.tensor_tensor(rstd[:, :], var_eps[:, :], minus_half[:, :], ALU.pow).then_inc(rstd_ready, 1)

            def ctx_max_of(c):
                pool.wait_ge(ctx_max_ready, c + 1)
                pool.sem_inc(pool_passed, 1)
                pool.partition_all_reduce(ctx_max_all[:, :], ctx_max[:, KB:KB + 1], P, REDUCE_MAX) \
                    .then_inc(ctx_max_all_ready, 1)

            def weight_max(n, a, b):
                pool.wait_ge(max_ready, n + 1)
                pool.partition_all_reduce(amax_all[:, a:b], amax[:, a:b], P, REDUCE_MAX) \
                    .then_inc(max_all_ready, 1)

            def attn_bound(m):
                pool.wait_ge(attn_squared, m + 1)
                pool.partition_all_reduce(amax_all[:, m:m + 1], amax[:, m:m + 1], P, REDUCE_MAX) \
                    .then_inc(pool_step, 1)
                pool.wait_ge(pool_step, m + 1)
                pool.tensor_tensor(amax_all[:, m:m + 1], amax_all[:, m:m + 1], half[:, 0:1], ALU.pow) \
                    .then_inc(attn_bounded, 1)

            rstd_of(0)
            for m in (K, V, Q):
                attn_bound(m)
            weight_max(0, M_SU, M_SU + 1)
            ctx_max_of(0)
            pool.wait_ge(norms_read, 1)
            pool.tensor_tensor(norms[:, :], norms[:, :], half[:, :], ALU.pow).then_inc(norms_ready, 1)
            weight_max(1, M_GATE, M_DOWN + 1)
            weight_max(2, M_COEF, M_COEF + 1)
            attn_bound(O)
            rstd_of(1)
            with pool.Fori(1, CHUNKS - 1) as c:
                ctx_max_of(c)
                rstd_of(c + 1)
            ctx_max_of(CHUNKS - 1)

        @block.scalar
        def _(act):
            def split_attn(m):
                for k in range(KB):
                    act.activation(w_attn[:, m, HI, k, :], raw_attn[m][:, k, :], ACT.Copy,
                                   scale=s_attn[:, m:m + 1]).then_inc(attn_hi, 1)

            def xt_high(c):
                for k in range(KB):
                    act.wait_ge(xp_done, 4 * c + k + 1)
                    act.activation(xt[:, HI, k, :], ring[k][:, :], ACT.Copy).then_inc(xt_hi, 1)

            def square_attn(m):
                act.wait_ge(attn_raw_loaded[m], 16)
                if m:
                    act.wait_ge(attn_squared, m)
                act.activation(unkept if m != O else unkept_o, flat_attn(m), ACT.Square, accum_out=amax[:, m:m + 1]) \
                    .then_inc(attn_squared, 1)

            def square(u):
                b, m = UNITS[u]
                raw = down_raw[:, 4 * b:4 * b + 4, :] if m is None else ug_raw[:, m, b, :, :]
                act.wait_ge(unit_loaded[u], 16)
                if u >= 2:
                    act.wait_ge(normed, u - 1)
                act.activation(squares[:, u % 2, :, :], raw, ACT.Square).then_inc(squared, 1)

            def evict_qkv(c, units=()):
                units = list(units)
                for f in range(KB):
                    for j, m in enumerate((K, V, Q)):
                        n = 3 * f + j
                        bank = ring[n % 4]
                        act.wait_ge(qkv_done, 12 * c + n + 1)
                        if n and units:
                            square(units.pop(0))
                        unscale = i_attn[:, m:m + 1]
                        if m == V:
                            if not (isinstance(c, int) and c == 0 and f == 0):
                                act.wait_ge(v_used, 4 * c + f)
                            act.activation(v_sb[:, :], bank[:, :], ACT.Identity,
                                           bias=vec[:, BV + f:BV + f + 1], scale=unscale).then_inc(v_evicted, 1)
                            continue
                        e, r, b, done = (e_k, r_k, BK, k_evicted) if m == K else (e_q, r_q, BQ, q_evicted)
                        if not (isinstance(c, int) and c == 0 and f == 0):
                            act.wait_ge(ctx_made, 4 * c + f)
                        act.activation(e[:, :], bank[:, :], ACT.Exp, bias=vec[:, b + f:b + f + 1], scale=unscale)
                        act.activation(r[:, :], bank[:, :], ACT.Relu, bias=vec[:, b + f:b + f + 1],
                                       scale=unscale).then_inc(done, 1)
                for u in units:
                    square(u)

            def split_part(b, m):
                for k in range(KB):
                    act.wait_ge(hada_done, part_at(b, m) + k + 1)
                    act.activation(ug[:, m, b, k, HI, :], ring[k][:, :], ACT.Copy,
                                   scale=coef_ug[:, m, k:k + 1]).then_inc(ffn_hi, 1)

            def silu_gates(c):
                first = isinstance(c, int) and c == 0
                for i in range(NI):
                    if first and i == 4:
                        act.wait_ge(coef_ready, 5)
                        split_down()
                        split_part(1, GATE)
                        split_part(1, UP)
                    act.wait_ge(gate_done, 16 * c + i + 1)
                    if not (isinstance(c, int) and c == 0 and i < 2):
                        act.wait_ge(up_read, 16 * c + i - 1)
                    act.activation(silu[:, i % 2, :], ring[(12 + 2 * i) % 4][:, :], ACT.Silu,
                                   scale=gate_out[:, i:i + 1]).then_inc(silu_ready, 1)
                    if first and i % 4 in (1, 2) and 1 <= i // 4 < BLOCKS - 1:
                        split_part(i // 4 + 1, i % 4 - 1)
                    if first and i == 8:
                        square_attn(O)
                    if first and i == 12:
                        act.wait_ge(coef_ready, 6)
                        split_attn(O)

            def silu_outs(c):
                for t in range(TB):
                    act.wait_ge(z_ready, 4 * c + t + 1)
                    act.activation(gate_g[:, t % 2, :], gate_g[:, t % 2, :], ACT.Silu).then_inc(gate_ready, 1)

            def split_down():
                for k in range(NI):
                    act.wait_ge(hada_done, 2 * KB + k + 1)
                    act.activation(down[:, k, HI, :], down_ps[k % 4][:, :], ACT.Copy,
                                   scale=coef_down[:, k:k + 1]).then_inc(ffn_hi, 1)

            for m in (K, V, Q):
                square_attn(m)
                if m == K:
                    xt_high(0)
            for m in (K, V, Q):
                act.wait_ge(coef_ready, m + 1)
                split_attn(m)
            act.wait_ge(consts_loaded, 48)
            evict_qkv(0, range(len(UNITS)))
            act.wait_ge(coef_ready, 4)
            split_part(0, GATE)
            split_part(0, UP)
            silu_gates(0)
            xt_high(1)
            silu_outs(0)
            with act.Fori(1, CHUNKS - 1) as c:
                evict_qkv(c)
                silu_gates(c)
                xt_high(c + 1)
                silu_outs(c)
            evict_qkv(CHUNKS - 1)
            silu_gates(CHUNKS - 1)
            silu_outs(CHUNKS - 1)

        @block.vector
        def _(dve):
            class Chain:

                def __init__(self, counter, base):
                    self.counter, self.base, self.n = counter, base, 0

                def after(self, ins):
                    self.n += 1
                    ins.then_inc(self.counter, 1)
                    dve.wait_ge(self.counter, self.base + self.n)

            prep = Chain(prep_step, 0)

            def pow2(chain, src, factor, scale, inverse, least=TINY):
                t = pw[:, 0:src.free_size()]
                chain.after(dve.tensor_scalar(t, src, factor, None, ALU.mult))
                chain.after(dve.tensor_scalar(t.bitcast(I32), t.bitcast(I32), EXPONENT, None, ALU.bitwise_and))
                chain.after(dve.tensor_scalar(inverse.bitcast(I32), t.bitcast(I32), float(least << 23),
                                              -float(TOP << 23), ALU.max, ALU.add))
                chain.after(dve.tensor_scalar(scale.bitcast(I32), inverse.bitcast(I32), -1.0,
                                              float(254 << 23), ALU.mult, ALU.add))

            def absmax(dst, src):
                return dve.tensor_reduce(dst, src, AX_X, ALU.max, apply_absolute_value=True)

            def flat(ap):
                return ap.rearrange("p k n -> p (k n)")

            def ln_stats(c, chain):
                dve.wait_ge(x_ln_loaded, 16 * c + 16)
                for t in range(TB):
                    last = dve.bn_stats(stats[:, t, :], x_ln[:, t, :])
                chain.after(last)
                dve.sem_inc(dve_passed, 1)
                for t in range(TB):
                    last = dve.bn_aggr(mean_var[:, t, :], stats[:, t, :])
                chain.after(last)
                dve.tensor_scalar(var_eps[:, :], mean_var[:, :, 1], EPS, None, ALU.add).then_inc(var_ready, 1)

            def ln_scale(c, chain):
                dve.wait_ge(rstd_ready, c + 1)
                chain.after(dve.tensor_scalar(rstd[:, :], rstd[:, :], X_SCALE, None, ALU.mult))

            def normalise(t):
                dve.tensor_scalar(x_ln[:, t, :], x_ln[:, t, :], mean_var[:, t, 0:1], rstd[:, t:t + 1],
                                  ALU.subtract, ALU.mult).then_inc(xn_ready, 1)

            def xt_low(c):
                for k in range(KB):
                    dve.wait_ge(xt_hi, 4 * c + k + 1)
                    dve.tensor_tensor(xt[:, LO, k, :], ring[k][:, :], xt[:, HI, k, :], ALU.subtract) \
                        .then_inc(xt_ready, 1)

            def attention(c, chain, between=()):
                for f in range(KB):
                    if 0 < f <= len(between):
                        between[f - 1]()
                    dve.wait_ge(k_evicted, 4 * c + f + 1)
                    chain.after(dve.scalar_tensor_tensor(e_k[:, :], e_k[:, :], 1.0, r_k[:, :], ALU.min, ALU.add))
                    dve.wait_ge(v_evicted, 4 * c + f + 1)
                    dve.tensor_tensor(e_k[:, :], e_k[:, :], v_sb[:, :], ALU.mult).then_inc(v_used, 1)
                    dve.wait_ge(v_used, 4 * c + f + 1)
                    dve.tensor_tensor_scan(r_k[:, :], e_k[:, :], e_k[:, :], 0.0, ALU.add, ALU.bypass)
                    dve.wait_ge(q_evicted, 4 * c + f + 1)
                    chain.after(dve.scalar_tensor_tensor(e_q[:, :], e_q[:, :], 1.0, r_q[:, :], ALU.min, ALU.add))
                    dve.tensor_tensor(ctx_f[:, f, :], e_q[:, :], r_k[:, :], ALU.mult).then_inc(ctx_made, 1)
                    dve.wait_ge(ctx_made, 4 * c + f + 1)
                    last = absmax(ctx_max[:, f:f + 1], ctx_f[:, f, :])
                chain.after(last)
                dve.tensor_reduce(ctx_max[:, KB:KB + 1], ctx_max[:, 0:KB], AX_X, ALU.max).then_inc(ctx_max_ready, 1)

            def ctx_scale(c, chain):
                dve.wait_ge(ctx_max_all_ready, c + 1)
                pow2(chain, ctx_max_all[:, 0:1], 1.0, s_c[:, :], i_c[:, :])
                if not (isinstance(c, int) and c == 0):
                    take_back_o(chain)

            def take_back_o(chain):
                chain.after(dve.tensor_scalar(o_out[:, :], i_c[:, :], i_attn[:, O:O + 1], HEAD_DIM ** -0.5,
                                              ALU.mult, ALU.mult))

            def split_ctx(f, chain):
                chain.after(dve.tensor_scalar(ctx_s[:, HI, f, :], ctx_f[:, f, :], s_c[:, 0:1], None, ALU.mult))
                dve.scalar_tensor_tensor(ctx_s[:, LO, f, :], ctx_f[:, f, :], s_c[:, 0:1], ctx_s[:, HI, f, :],
                                         ALU.mult, ALU.subtract).then_inc(ctx_split, 1)

            def hidden(c, i, chain):
                dve.wait_ge(silu_ready, 16 * c + i + 1)
                dve.wait_ge(up_done, 16 * c + i + 1)
                if not (isinstance(c, int) and c == 0 and i == 0):
                    dve.wait_ge(h_ready, 16 * c + i)
                dve.scalar_tensor_tensor(h_f, ring[(13 + 2 * i) % 4][:, :], up_out[:, i:i + 1], silu[:, i % 2, :],
                                         ALU.mult, ALU.mult).then_inc(up_read, 1)
                dve.wait_ge(up_read, 16 * c + i + 1)
                if not (isinstance(c, int) and c == 0 and i < 2):
                    dve.wait_ge(down_step, 16 * c + i - 1)
                chain.after(dve.tensor_copy(h_s[:, i % 2, HI, :], h_f))
                dve.tensor_tensor(h_s[:, i % 2, LO, :], h_f, h_s[:, i % 2, HI, :], ALU.subtract).then_inc(h_ready, 1)

            def gate_argument(c, t):
                if t == 0:
                    dve.wait_ge(down_step, 16 * c + 16)
                dve.scalar_tensor_tensor(gate_g[:, t % 2, :], down_ps[t][:, :], i_d[:, 0:1], ws_dp_row,
                                         ALU.mult, ALU.mult).then_inc(z_ready, 1)

            def outputs(c, chain):
                gate_argument(c, 0)
                gate_argument(c, 1)
                for t in range(TB):
                    dve.wait_ge(o_done, 4 * c + t + 1)
                    if not (isinstance(c, int) and c == 0 and t == 0):
                        dve.wait_ge(out_ready, 4 * c + t)
                    dve.scalar_tensor_tensor(s_f, ring[t][:, :], o_out[:, 0:1], bo_row, ALU.mult, ALU.add) \
                        .then_inc(o_read, 1)
                    dve.wait_ge(o_read, 4 * c + t + 1)
                    dve.wait_ge(gate_ready, 4 * c + t + 1)
                    chain.after(dve.tensor_tensor(s_f, s_f, gate_g[:, t % 2, :], ALU.mult))
                    if t + 2 < TB:
                        gate_argument(c, t + 2)
                    if t == 0:
                        dve.wait_ge(x_res_loaded, 16 * c + 16)
                    dve.tensor_tensor(x_res[:, t, :], x_res[:, t, :], s_f, ALU.add).then_inc(out_ready, 1)

            def feed_forward(c, chain, last):
                for i in range(NI):
                    hidden(c, i, chain)
                    if i == 1:
                        ctx_scale(c, chain)
                    if 2 <= i < 2 + KB:
                        split_ctx(i - 2, chain)
                    if not last and i == 6:
                        ln_stats(c + 1, chain)
                    if not last and i == 8:
                        ln_scale(c + 1, chain)
                    if not last and 9 <= i < 9 + TB:
                        normalise(i - 9)
                if not last:
                    xt_low(c + 1)
                outputs(c, chain)

            def first_feed_forward(chain):
                for i in range(4, NI):
                    hidden(0, i, chain)
                    if i % 4 == 0 and i // 4 < BLOCKS - 1:
                        fly_part(i // 4 + 1, GATE)
                        fly_part(i // 4 + 1, UP)
                    if i % 4 in (1, 2) and i // 4 < BLOCKS - 1:
                        split_part(i // 4 + 1, i % 4 - 1)
                    if i == 7:
                        ctx_scale(0, chain)
                    if i == 10:
                        ln_stats(1, chain)
                    if i == 11:
                        prepare_o()
                        ln_scale(1, chain)
                    if 11 <= i < 11 + KB:
                        split_ctx(i - 11, chain)
                    if i == 12:
                        split_attn(O)
                    if i >= 12:
                        normalise(i - 12)
                xt_low(1)
                outputs(0, chain)

            def weight_scale(m):
                dve.wait_ge(attn_bounded, m + 1)
                pow2(prep, amax_all[:, m:m + 1], MARGIN, s_attn[:, m:m + 1], i_attn[:, m:m + 1], TINY_ROOT)
                dve.tensor_scalar(i_attn[:, m:m + 1], i_attn[:, m:m + 1], 1.0 if m == O else 1.0 / X_SCALE,
                                  None, ALU.mult).then_inc(coef_ready, 1)

            def split_attn(m):
                for k in range(KB):
                    dve.wait_ge(attn_hi, 4 * m + k + 1)
                    dve.scalar_tensor_tensor(w_attn[:, m, LO, k, :], raw_attn[m][:, k, :], s_attn[:, m:m + 1],
                                             w_attn[:, m, HI, k, :], ALU.mult, ALU.subtract).then_inc(attn_split, 1)

            def prepare_o():
                weight_scale(O)
                dve.wait_ge(coef_ready, 6)
                take_back_o(prep)

            def butterfly(src, dst, half):
                a = src.rearrange("p (a two b) n -> p a two b n", two=2, b=half)
                d = dst.rearrange("p (a two b) n -> p a two b n", two=2, b=half)
                dve.tensor_tensor(d[:, :, 0], a[:, :, 0], a[:, :, 1], ALU.add)
                return dve.tensor_tensor(d[:, :, 1], a[:, :, 0], a[:, :, 1], ALU.subtract)

            fly_rows = fly.rearrange("p (k n) -> p k n", k=KB)
            fly_cols = fly.rearrange("p (k n) -> p k n", k=NI)

            def fly_columns(g):
                cols = down_raw[:, :, g * P:(g + 1) * P]
                prep.after(butterfly(cols, fly_cols, 4))
                prep.after(butterfly(fly_cols, cols, 8))

            def fly_four(raw, done):
                if done:
                    dve.wait_ge(flown, done)
                prep.after(butterfly(raw, fly_rows, 1))
                butterfly(fly_rows, raw, 2).then_inc(flown, 1)

            def fly_part(b, m):
                fly_four(ug_raw[:, m, b, :, :], part_at(b, m) // KB)

            def fly_down(g):
                fly_four(down_raw[:, KB * g:KB * g + KB, :], 2 + g)

            def split_down(g):
                for k in range(KB * g, KB * g + KB):
                    dve.wait_ge(ffn_hi, 2 * KB + k + 1)
                    dve.scalar_tensor_tensor(down[:, k, LO, :], down_ps[k % 4][:, :], coef_down[:, k:k + 1],
                                             down[:, k, HI, :], ALU.mult, ALU.subtract).then_inc(ffn_split, 1)

            def split_part(b, m):
                for k in range(KB):
                    n = part_at(b, m) + k
                    dve.wait_ge(ffn_hi, n + 1)
                    dve.scalar_tensor_tensor(ug[:, m, b, k, LO, :], ring[k][:, :], coef_ug[:, m, k:k + 1],
                                             ug[:, m, b, k, HI, :], ALU.mult, ALU.subtract).then_inc(ffn_split, 1)

            dve.memset(ones[:, :], 1.0).then_inc(ones_set, 1)
            ln_stats(0, prep)
            ln_scale(0, prep)
            for t in range(TB):
                normalise(t)
            xt_low(0)
            for m in (K, V, Q):
                weight_scale(m)
                split_attn(m)
            dve.wait_ge(consts_loaded, 48)
            absmax(amax[:, M_SU:M_SU + 1], vec[:, SU_UG:SU_UG + KB]).then_inc(max_ready, 1)

            def columns(g):
                for u in range(2, 2 + GROUPS):
                    dve.wait_ge(unit_loaded[u], 16)
                dve.wait_ge(squared, 2 + GROUPS)
                fly_columns(g)

            def part(m):
                dve.wait_ge(unit_loaded[m], 16)
                dve.wait_ge(squared, m + 1)
                fly_part(0, m)

            chain = Chain(dve_step, 0)
            attention(0, chain, (lambda: part(GATE), lambda: part(UP), lambda: columns(0)))

            dve.wait_ge(normed, len(UNITS))
            n_ps = down_ps[0]
            prep.after(dve.tensor_copy(norms[:, 0:2 * NI], n_ps[:, 0:2 * NI]))
            prep.after(dve.tensor_reduce(norms[:, 2 * NI:ROOTS],
                                         n_ps[:, 2 * NI:2 * NI + 16].rearrange("p (g n) -> p n g", g=GROUPS),
                                         AX_X, ALU.add))
            dve.tensor_scalar(norms[:, :], norms[:, :], MARGIN, TINY_SQUARE, ALU.mult, ALU.max).then_inc(norms_read, 1)
            columns(1)
            dve.wait_ge(norms_ready, 1)
            prep.after(dve.tensor_reduce(amax[:, M_GATE:M_UP + 1], norms[:, 0:2 * NI].rearrange("p (m i) -> p m i", m=2),
                                         AX_X, ALU.max))
            dve.tensor_reduce(amax[:, M_DOWN:M_DOWN + 1], norms[:, 2 * NI:ROOTS], AX_X, ALU.max).then_inc(max_ready, 1)
            dve.wait_ge(max_all_ready, 1)
            prep.after(dve.tensor_tensor(su2[:, :], amax_all[:, M_SU:M_SU + 1], amax_all[:, M_SU:M_SU + 1], ALU.mult))
            prep.after(dve.tensor_tensor(bound[:, :], vec[:, WS_GATE:WS_GATE + NI], vec[:, WS_UP:WS_UP + NI], ALU.mult))
            prep.after(dve.tensor_scalar(bound[:, :], bound[:, :], su2[:, 0:1], float(D), ALU.mult, ALU.mult))
            prep.after(dve.tensor_tensor(bound[:, :], bound[:, :], norms[:, 0:NI], ALU.mult))
            prep.after(dve.tensor_tensor(bound[:, :], bound[:, :], norms[:, NI:2 * NI], ALU.mult))
            pow2(prep, bound[:, :], 1.0, s_h[:, :], i_h[:, :])
            prep.after(dve.tensor_tensor(coef_down[:, :], vec[:, SU_DP:SU_DP + NI], i_h[:, :], ALU.mult))
            absmax(amax[:, M_COEF:M_COEF + 1], coef_down[:, :]).then_inc(max_ready, 1)
            dve.wait_ge(max_all_ready, 2)
            prep.after(dve.tensor_scalar(pw[:, 2:4], amax_all[:, M_GATE:M_UP + 1], amax_all[:, M_SU:M_SU + 1],
                                         None, ALU.mult))
            pow2(prep, pw[:, 2:4], D ** 0.5, s_ug[:, :], i_ug[:, :])
            for m, w in ((GATE, WS_GATE), (UP, WS_UP)):
                prep.after(dve.tensor_scalar(coef_ug[:, m, :], vec[:, SU_UG:SU_UG + KB], s_ug[:, m:m + 1],
                                             None, ALU.mult))
                dst = gate_out if m == GATE else up_out
                prep.after(dve.tensor_scalar(dst[:, :], vec[:, w:w + NI], i_ug[:, m:m + 1],
                                             D ** -0.5 / X_SCALE, ALU.mult, ALU.mult))
            dve.tensor_tensor(up_out[:, :], up_out[:, :], s_h[:, :], ALU.mult).then_inc(coef_ready, 1)
            dve.wait_ge(coef_ready, 4)
            split_part(0, GATE)
            split_part(0, UP)
            dve.wait_ge(max_all_ready, 3)
            prep.after(dve.tensor_tensor(pw[:, 4:5], amax_all[:, M_COEF:M_COEF + 1],
                                         amax_all[:, M_DOWN:M_DOWN + 1], ALU.mult))
            pow2(prep, pw[:, 4:5], F ** 0.5, s_d[:, :], i_d[:, :])
            prep.after(dve.tensor_scalar(coef_down[:, :], coef_down[:, :], s_d[:, 0:1], None, ALU.mult))
            dve.tensor_scalar(i_d[:, :], i_d[:, :], F ** -0.5, None, ALU.mult).then_inc(coef_ready, 1)
            columns(2)
            hidden(0, 0, chain)
            columns(3)
            hidden(0, 1, chain)
            for g in range(GROUPS):
                fly_down(g)
                if g:
                    split_down(g - 1)
            fly_part(1, GATE)
            split_down(GROUPS - 1)
            hidden(0, 2, chain)
            hidden(0, 3, chain)
            split_part(1, GATE)
            fly_part(1, UP)
            split_part(1, UP)

            first_feed_forward(chain)
            before = chain.n
            steps = before + 1
            with dve.Fori(1, CHUNKS - 1) as c:
                chain = Chain(dve_step, c * steps - (steps - before))
                attention(c, chain)
                feed_forward(c, chain, False)
                assert chain.n == steps
            chain = Chain(dve_step, (CHUNKS - 1) * steps - (steps - before))
            attention(CHUNKS - 1, chain)
            feed_forward(CHUNKS - 1, chain, True)

        @block.tensor
        def _(pe):
            def product(bank, pairs):
                for n, (lhs, rhs) in enumerate(pairs):
                    mm = pe.matmul(bank[:, :], lhs, rhs, start=(n == 0), stop=(n == len(pairs) - 1))
                return mm

            def transposes(c):
                pe.wait_ge(xn_ready, 4 * c + 4)
                for k in range(KB):
                    if not (isinstance(c, int) and c == 0):
                        if k % 2 == 0:
                            pe.wait_ge(silu_ready, 16 * c - 1 + k // 2)
                        else:
                            pe.wait_ge(up_read, 16 * c - 1 + k // 2)
                    for t in range(TB):
                        mm = pe.transpose(ring[k][:, t * P:(t + 1) * P], x_ln[:, t, k * P:(k + 1) * P], ident[:, :])
                    mm.then_inc(xp_done, 1)

            def norm(u):
                b, m = UNITS[u]
                at = 2 * NI + 4 * b if m is None else m * NI + 4 * b
                pe.wait_ge(squared, u + 1)
                for n in range(4):
                    for k in range(KB):
                        mm = pe.matmul(down_ps[0][:, at + n:at + n + 1], squares[:, u % 2, k, n * P:(n + 1) * P],
                                       ones[:, :], start=(k == 0), stop=(k == KB - 1))
                mm.then_inc(normed, 1)

            def qkv(c, units=()):
                units = list(units)
                pe.wait_ge(xt_ready, 4 * c + 4)
                for f in range(KB):
                    for j, m in enumerate((K, V, Q)):
                        n = 3 * f + j
                        if n < 4:
                            if not (isinstance(c, int) and c == 0):
                                pe.wait_ge(o_read, 4 * c - 4 + n + 1)
                        else:
                            before = (n - 4) // 3
                            pe.wait_ge((k_evicted, v_evicted, q_evicted)[(n - 4) % 3], 4 * c + before + 1)
                        if isinstance(c, int) and c == 0 and f == 0:
                            pe.wait_ge(attn_split, 4 * j + 4)
                        cols = slice(f * P, (f + 1) * P)
                        pairs = []
                        for k in range(KB):
                            w_hi, w_lo = w_attn[:, m, HI, k, cols], w_attn[:, m, LO, k, cols]
                            pairs += [(w_hi, xt[:, HI, k, :]), (w_hi, xt[:, LO, k, :]), (w_lo, xt[:, HI, k, :])]
                        product(ring[n % 4], pairs).then_inc(qkv_done, 1)
                        if n >= 2 and units:
                            norm(units.pop(0))
                for u in units:
                    norm(u)

            def gate_or_up(c, i, m):
                n = 2 * i + m
                first = isinstance(c, int) and c == 0
                b = i // 4
                if first and i < 2:
                    pe.wait_ge(ffn_split, part_at(0, UP) + KB)
                elif first and i == 5:
                    pe.wait_ge(ffn_split, part_at(1, UP) + 2 + m + 1)
                elif first and i % 4 == 0:
                    pe.wait_ge(ffn_split, part_at(b, UP) + (KB if m == UP else 1))
                elif first and i % 4 == 2 and 1 <= b < BLOCKS - 1:
                    pe.wait_ge(ffn_split, part_at(b + 1, GATE) + m + 1)
                elif first and i % 4 == 3 and 1 <= b < BLOCKS - 1:
                    pe.wait_ge(ffn_split, part_at(b + 1, UP) + 2 + m + 1)
                elif n < 4:
                    pe.wait_ge((k_evicted, v_evicted, q_evicted)[(8 + n) % 3], 4 * c + (8 + n) // 3 + 1)
                else:
                    pe.wait_ge(silu_ready if m == GATE else up_read, 16 * c + i - 1)
                cols = slice(i % 4 * P, (i % 4 + 1) * P)
                pairs = []
                for k in range(KB):
                    w_hi, w_lo = ug[:, m, i // 4, k, HI, cols], ug[:, m, i // 4, k, LO, cols]
                    pairs += [(w_hi, xt[:, HI, k, :]), (w_hi, xt[:, LO, k, :]), (w_lo, xt[:, HI, k, :])]
                product(ring[(12 + n) % 4], pairs).then_inc(gate_done if m == GATE else up_done, 1)

            def down_product(c, i):
                if i == 0:
                    if isinstance(c, int) and c == 0:
                        pe.wait_ge(ffn_split, 2 * KB + NI)
                    else:
                        pe.wait_ge(gate_ready, 4 * c)
                pe.wait_ge(h_ready, 16 * c + i + 1)
                for t in range(TB):
                    cols = slice(t * P, (t + 1) * P)
                    pairs = ((h_s[:, i % 2, HI, cols], down[:, i, HI, :]), (h_s[:, i % 2, HI, cols], down[:, i, LO, :]),
                             (h_s[:, i % 2, LO, cols], down[:, i, HI, :]))
                    for n, (lhs, rhs) in enumerate(pairs):
                        mm = pe.matmul(down_ps[t][:, :], lhs, rhs, start=(i == 0 and n == 0),
                                       stop=(i == NI - 1 and n == 2))
                mm.then_inc(down_step, 1)

            def out_product(c, last):
                pe.wait_ge(ctx_split, 4 * c + 4)
                if isinstance(c, int) and c == 0:
                    pe.wait_ge(attn_split, 16)
                for t in range(TB):
                    if not last:
                        pe.wait_ge(xt_ready, 4 * c + 4 + t + 1)
                    elif t % 2 == 0:
                        pe.wait_ge(silu_ready, 16 * c + 15 + t // 2)
                    else:
                        pe.wait_ge(up_read, 16 * c + 15 + t // 2)
                    cols = slice(t * P, (t + 1) * P)
                    pairs = []
                    for f in range(KB):
                        c_hi, c_lo = ctx_s[:, HI, f, cols], ctx_s[:, LO, f, cols]
                        pairs += [(c_hi, w_attn[:, O, HI, f, :]), (c_hi, w_attn[:, O, LO, f, :]),
                                  (c_lo, w_attn[:, O, HI, f, :])]
                    product(ring[t], pairs).then_inc(o_done, 1)

            def hadamard(b, m):
                pe.wait_ge(flown, part_at(b, m) // KB + 1)
                for k in range(KB):
                    if b == 0 and m == GATE:
                        pe.wait_ge(q_evicted, KB)
                    elif b == 1 and m == GATE:
                        pe.wait_ge((silu_ready, up_read)[k % 2], 2 + k // 2 + 1)
                    elif b <= 1 or (m == UP and k >= 2):
                        pe.wait_ge(ffn_split, part_at(b, GATE) + k + 1)
                    else:
                        pe.wait_ge((silu_ready, up_read)[k % 2], 4 * (b - 1) + (2 if m == UP else k // 2) + 1)
                    pe.matmul(ring[k][:, :], hada[:, :], ug_raw[:, m, b, k, :], start=True, stop=True) \
                        .then_inc(hada_done, 1)

            def hadamard_down():
                for g in range(GROUPS):
                    pe.wait_ge(flown, 2 + g + 1)
                    for k in range(KB):
                        if g:
                            pe.wait_ge(ffn_split, 2 * KB + (g - 1) * KB + k + 1)
                        pe.matmul(down_ps[k][:, :], hada[:, :], down_raw[:, KB * g + k, :], start=True, stop=True) \
                            .then_inc(hada_done, 1)

            def feed_forward(c, last):
                for i in range(NI):
                    gate_or_up(c, i, GATE)
                    gate_or_up(c, i, UP)
                    if i >= 1:
                        down_product(c, i - 1)
                if not last:
                    transposes(c + 1)
                down_product(c, NI - 1)
                out_product(c, last)

            def first_feed_forward():
                for i in range(4):
                    gate_or_up(0, i, GATE)
                    gate_or_up(0, i, UP)
                hadamard_down()
                down_product(0, 0)
                down_product(0, 1)
                hadamard(1, GATE)
                down_product(0, 2)
                hadamard(1, UP)
                down_product(0, 3)
                for i in range(4, NI):
                    gate_or_up(0, i, GATE)
                    gate_or_up(0, i, UP)
                    if i >= 5:
                        down_product(0, i - 1)
                    if i % 4 in (1, 2) and i // 4 < BLOCKS - 1:
                        hadamard(i // 4 + 1, i % 4 - 1)
                transposes(1)
                down_product(0, NI - 1)
                out_product(0, False)

            pe.wait_ge(ident_loaded, 16)
            transposes(0)
            pe.wait_ge(ones_set, 1)
            qkv(0, range(len(UNITS)))
            pe.wait_ge(consts_loaded, 48)
            pe.wait_ge(norms_read, 1)
            hadamard(0, GATE)
            hadamard(0, UP)
            first_feed_forward()
            with pe.Fori(1, CHUNKS - 1) as c:
                qkv(c)
                feed_forward(c, False)
            qkv(CHUNKS - 1)
            feed_forward(CHUNKS - 1, True)


def kernel(**inputs):
    import numpy as np
    import concourse.bacc as bacc
    from concourse.bass_utils import run_bass_kernel_spmd

    def part(name):
        return np.asarray(inputs[name])

    def by_partition(v):
        return np.asarray(v).reshape(-1, P).T

    hadamard = np.ones((1, 1), np.float32)
    while hadamard.shape[0] < P:
        hadamard = np.block([[hadamard, hadamard], [hadamard, -hadamard]])
    ws_ug = part("L0_ffn_Wscale_ug")
    arrays = {
        "x": part("L0_attn_x"),
        "wk_t": part("L0_attn_Wk").T, "wv_t": part("L0_attn_Wv").T, "wq_t": part("L0_attn_Wq").T,
        "wo_t": part("L0_attn_Wo").T,
        "gate_t": part("L0_ffn_W_gate").T, "up_t": part("L0_ffn_W_up").T, "down_t": part("L0_ffn_W_down").T,
        "vecs": np.concatenate([by_partition(v) for v in (
            part("L0_attn_bk"), part("L0_attn_bv"), part("L0_attn_bq"), part("L0_ffn_SU_ug"),
            part("L0_ffn_SU_dp"), ws_ug[F:], ws_ug[:F])], axis=1),
        "rows": np.stack([part("L0_attn_bo"), part("L0_ffn_Wscale_dp")]),
        "ident": np.eye(P, dtype=np.float32),
        "hadamard": hadamard,
    }
    arrays = {f"in_{k}": np.ascontiguousarray(v) for k, v in arrays.items()}
    nc = bacc.Bacc("TRN2", target_bir_lowering=False, num_devices=1)
    args = [nc.dram_tensor(k, v.shape, mybir.dt.from_np(v.dtype), kind="ExternalInput").ap()
            for k, v in arrays.items()]
    args.append(nc.dram_tensor("out", (CHUNKS, T, D), F32, kind="ExternalOutput").ap())
    build(nc, *args)
    r = run_bass_kernel_spmd(nc, [arrays], core_ids=[0])
    return r.results[0]["out"]
```

```python
from contextlib import ExitStack

import concourse.bass as bass
from concourse import mybir

F32 = mybir.dt.float32
F16 = mybir.dt.float16
BF16 = mybir.dt.bfloat16
I32 = mybir.dt.int32
ALU = mybir.AluOpType
ACT = mybir.ActivationFunctionType
AX_X = mybir.AxisListType.X
REDUCE_MAX = bass.bass_isa.ReduceOp.max

P = 128
CHUNKS, T, D = 8, 512, 512
F = 2048
HEAD_DIM = D // 16
KB = D // P
TB = T // P
NI = F // P
BLOCKS = F // 512
EPS = 1e-5

X_SCALE = 1024.0
TOP = 14
TINY = 27
TINY_ROOT = 77
TINY_SQUARE = 2.0 ** -100
EXPONENT = 0x7F800000

BK, BV, BQ, SU_UG, SU_DP, WS_GATE, WS_UP = 0, 4, 8, 12, 16, 32, 48
VECS = 64
K, V, Q, O = range(4)
SQUARED = (K, Q, O)
M_SU, M_GATE, M_UP, M_DOWN, M_COEF = range(4, 9)
MAXIMA = 9
GATE, UP = 0, 1
UNITS = [(b, m) for b in range(BLOCKS) for m in (GATE, UP)]
GROUPS = NI // KB
EARLY = 2
AHEAD = EARLY * KB
MARGIN = 1.02
HI, LO = 0, 1


def build(nc, x, wk_t, wv_t, wq_t, wo_t, gate_t, up_t, down_t, vecs, rows, ident_in, hada_in, out):
    with ExitStack() as ctx:
        def sb(name, shape, dt=F32):
            return ctx.enter_context(nc.sbuf_tensor(name, shape, dt))

        def sem(name):
            return ctx.enter_context(nc.semaphore(name))

        w_attn = sb("w_attn", [P, 4, 2, KB, D], F16)
        w_ug = sb("w_ug", [P, 2 * BLOCKS * KB * 512])
        w_down = sb("w_down", [P, NI * D])
        ug_raw = w_ug[:, :].rearrange("p (m b k n) -> p m b k n", m=2, b=BLOCKS, k=KB)
        ug = w_ug[:, :].bitcast(F16).rearrange("p (m b k s n) -> p m b k s n", m=2, b=BLOCKS, k=KB, s=2)
        down_raw = w_down[:, :].rearrange("p (k n) -> p k n", k=NI)
        down = w_down[:, :].bitcast(F16).rearrange("p (k s n) -> p k s n", k=NI, s=2)

        x_ln = sb("x_ln", [P, TB, D])
        x_res = sb("x_res", [P, TB, D])
        xt = sb("xt", [P, 2, KB, T], F16)
        e_k, r_k = sb("e_k", [P, T]), sb("r_k", [P, T])
        e_q, r_q = sb("e_q", [P, T]), sb("r_q", [P, T])
        v_sb = sb("v_sb", [P, T])
        ctx_f = sb("ctx_f", [P, KB, T])
        ctx_s = sb("ctx_s", [P, 2, KB, T], F16)
        scratch = sb("scratch", [P, 4096])
        silu = scratch[:, 0:1024].rearrange("p (r n) -> p r n", r=2)
        gate_g = scratch[:, 1024:2048].rearrange("p (r n) -> p r n", r=2)
        h_s = scratch[:, 2048:3072].bitcast(F16).rearrange("p (r s n) -> p r s n", r=2, s=2)
        h_first = ctx_s[:, :, :, :].rearrange("p s k n -> p (s k n)").rearrange("p (r s n) -> p r s n", r=KB, s=2)
        h_f = scratch[:, 3072:3584]
        s_f = scratch[:, 3584:4096]
        squares = scratch[:, 0:2048].bitcast(BF16).rearrange("p (r k n) -> p r k n", r=2, k=KB)
        unkept = scratch[:, 2048:3072].bitcast(BF16)
        unkept_down = scratch[:, 3072:4096].bitcast(BF16)
        unkept_o = ctx_s[:, 0, :, :].rearrange("p k n -> p (k n)").bitcast(BF16)
        fly = x_ln[:, :, :].rearrange("p t n -> p (t n)")
        raw_attn = [ctx_f[:, :, :],
                    ctx_s[:, :, :, :].rearrange("p s k n -> p (s k n)").bitcast(F32)
                    .rearrange("p (k n) -> p k n", k=KB),
                    x_res[:, :, :], x_res[:, :, :]]

        vec = sb("vec", [P, VECS])
        row = sb("row", [P, 2, D])
        bo_row, ws_dp_row = row[:, 0, :], row[:, 1, :]
        ident = sb("ident", [P, P])
        hada = sb("hada", [P, P])
        amax = sb("amax", [P, MAXIMA])
        amax_all = sb("amax_all", [P, MAXIMA])
        norms = sb("norms", [P, 2 * NI])
        down_sums = sb("down_sums", [P, GROUPS])
        half = sb("half", [P, 2 * NI])
        ones = sb("ones", [P, 1], BF16)
        pw = sb("pw", [P, NI])
        s_attn, i_attn = sb("s_attn", [P, 4]), sb("i_attn", [P, 4])
        s_ug, i_ug = sb("s_ug", [P, 2]), sb("i_ug", [P, 2])
        coef_ug = sb("coef_ug", [P, 2, KB])
        bound = sb("bound", [P, NI])
        s_h, i_h = sb("s_h", [P, NI]), sb("i_h", [P, NI])
        gate_out = sb("gate_out", [P, NI])
        up_out = sb("up_out", [P, NI])
        coef_down = sb("coef_down", [P, NI])
        s_d, i_d = sb("s_d", [P, 1]), sb("i_d", [P, 1])
        su2 = sb("su2", [P, 1])
        stats = sb("stats", [P, TB, 6])
        mean_var = sb("mean_var", [P, TB, 2])
        var_eps, rstd = sb("var_eps", [P, TB]), sb("rstd", [P, TB])
        minus_half = sb("minus_half", [P, TB])
        ctx_max, ctx_max_all = sb("ctx_max", [P, KB + 1]), sb("ctx_max_all", [P, 1])
        s_c, i_c, o_out = sb("s_c", [P, 1]), sb("i_c", [P, 1]), sb("o_out", [P, 1])

        ring = [ctx.enter_context(nc.psum_tensor(f"ring{i}", [P, 512], F32)) for i in range(4)]
        down_ps = [ctx.enter_context(nc.psum_tensor(f"down{i}", [P, 512], F32)) for i in range(TB)]

        ident_loaded, consts_loaded = sem("ident_loaded"), sem("consts_loaded")
        attn_raw_loaded = [sem(f"attn_raw_loaded{m}") for m in range(4)]
        x_first_loaded = [sem(f"x_first_loaded{t}") for t in range(TB)]
        down_loaded = [sem(f"down_loaded{g}") for g in range(GROUPS)]
        down_squared, down_bounded = sem("down_squared"), sem("down_bounded")
        unit_loaded = [sem(f"unit_loaded{u}") for u in range(len(UNITS))]
        x_ln_loaded, x_res_loaded, out_stored = sem("x_ln_loaded"), sem("x_res_loaded"), sem("out_stored")
        prep_step = sem("prep_step")
        dve_step = sem("dve_step")
        halves_set, ones_set = sem("halves_set"), sem("ones_set")
        attn_squared = sem("attn_squared")
        squared, normed = sem("squared"), sem("normed")
        norms_read, norms_ready = sem("norms_read"), sem("norms_ready")
        pool_passed, dve_passed = sem("pool_passed"), sem("dve_passed")
        max_ready, max_all_ready = sem("max_ready"), sem("max_all_ready")
        attn_bounded, pool_step = sem("attn_bounded"), sem("pool_step")
        attn_hi, attn_split = sem("attn_hi"), sem("attn_split")
        flown = sem("flown")
        hada_done, ffn_hi, ffn_split = sem("hada_done"), sem("ffn_hi"), sem("ffn_split")
        coef_ready = sem("coef_ready")
        var_ready, rstd_ready = sem("var_ready"), sem("rstd_ready")
        xn_ready, xp_done, xt_hi, xt_ready = sem("xn_ready"), sem("xp_done"), sem("xt_hi"), sem("xt_ready")
        qkv_done = sem("qkv_done")
        k_evicted, v_evicted, q_evicted = sem("k_evicted"), sem("v_evicted"), sem("q_evicted")
        v_used, ctx_made = sem("v_used"), sem("ctx_made")
        ctx_max_ready, ctx_max_all_ready, ctx_split = sem("ctx_max_ready"), sem("ctx_max_all_ready"), sem("ctx_split")
        gate_done, up_done = sem("gate_done"), sem("up_done")
        silu_ready, up_read, h_ready, down_step = sem("silu_ready"), sem("up_read"), sem("h_ready"), sem("down_step")
        z_ready, gate_ready = sem("z_ready"), sem("gate_ready")
        o_done, o_read, out_ready = sem("o_done"), sem("o_read"), sem("out_ready")

        def flat_attn(m):
            return raw_attn[m].rearrange("p k n -> p (k n)")

        def is_first(c):
            return isinstance(c, int) and c == 0

        block = ctx.enter_context(nc.Block())

        def part_at(b, m):
            return (2 * b + m) * KB + (NI if b >= EARLY else 0)

        def early_bank(n):
            return (down_ps if n < DOWN_AT + NI // 2 else ring)[n % 4]

        def h_slot(c, i):
            return h_first[:, i] if is_first(c) and i < KB else h_s[:, i % 2]

        DOWN_AT = part_at(EARLY - 1, UP) + KB

        def tokens(i):
            return x[i, :, :].rearrange("(t p) d -> p t d", p=P)

        @block.sync
        def _(sp):
            def load_x_ln(c):
                sp.dma_start(x_ln[:, :, :], tokens(c)).then_inc(x_ln_loaded, 16)

            def load_x_res(c):
                sp.dma_start(x_res[:, :, :], tokens(c)).then_inc(x_res_loaded, 16)

            def store(c):
                for t in range(TB):
                    sp.wait_ge(out_ready, 4 * c + t + 1)
                    sp.dma_start(out[c, t * P:(t + 1) * P, :], x_res[:, t, :]).then_inc(out_stored, 16)
                sp.wait_ge(out_stored, 64 * c + 64)

            def load_attn(m, w):
                sp.dma_start(raw_attn[m], w.rearrange("(k p) n -> p k n", p=P)).then_inc(attn_raw_loaded[m], 16)

            for t in range(TB):
                sp.dma_start(x_ln[:, t, :], x[0, t * P:(t + 1) * P, :]).then_inc(x_first_loaded[t], 16)
            sp.dma_start(ident[:, :], ident_in).then_inc(ident_loaded, 16)
            load_attn(K, wk_t)
            sp.dma_start(vec[:, :], vecs).then_inc(consts_loaded, 16)
            load_attn(V, wv_t)
            load_attn(Q, wq_t)
            sp.dma_start(hada[:, :], hada_in).then_inc(consts_loaded, 16)
            sp.dma_start(row[:, :, :], rows.partition_broadcast(P)).then_inc(consts_loaded, 16)
            for u, (b, m) in enumerate(UNITS):
                src = (gate_t, up_t)[m][:, b * 512:(b + 1) * 512]
                sp.dma_start(ug_raw[:, m, b, :, :], src.rearrange("(k p) n -> p k n", p=P)) \
                    .then_inc(unit_loaded[u], 16)
            for g in range(GROUPS):
                src = down_t[g * 512:(g + 1) * 512, :]
                sp.dma_start(down_raw[:, KB * g:KB * g + KB, :], src.rearrange("(k p) n -> p k n", p=P)) \
                    .then_inc(down_loaded[g], 16)
            sp.wait_ge(attn_split, 12)
            load_attn(O, wo_t)
            sp.wait_ge(flown, len(UNITS) + GROUPS)
            load_x_ln(1)
            sp.wait_ge(attn_split, 16)
            load_x_res(0)
            with sp.Fori(0, CHUNKS - 2) as c:
                sp.wait_ge(xp_done, 4 * c + 8)
                load_x_ln(c + 2)
                store(c)
                load_x_res(c + 1)
            store(CHUNKS - 2)
            load_x_res(CHUNKS - 1)
            store(CHUNKS - 1)

        @block.gpsimd
        def _(pool):
            pool.memset(minus_half[:, :], -0.5).then_inc(halves_set, 1)
            pool.memset(half[:, :], 0.5).then_inc(halves_set, 1)
            pool.wait_ge(halves_set, 2)

            def rstd_of(n):
                pool.wait_ge(var_ready, n + 1)
                pool.tensor_tensor(rstd[:, :], var_eps[:, :], minus_half[:, :], ALU.pow).then_inc(rstd_ready, 1)

            def ctx_max_of(c):
                pool.wait_ge(ctx_max_ready, c + 1)
                pool.sem_inc(pool_passed, 1)
                pool.partition_all_reduce(ctx_max_all[:, :], ctx_max[:, KB:KB + 1], P, REDUCE_MAX) \
                    .then_inc(ctx_max_all_ready, 1)

            def weight_max(n, a, b):
                pool.wait_ge(max_ready, n + 1)
                pool.partition_all_reduce(amax_all[:, a:b], amax[:, a:b], P, REDUCE_MAX) \
                    .then_inc(max_all_ready, 1)

            def attn_bound(m):
                n = SQUARED.index(m) + 1
                pool.wait_ge(attn_squared, n)
                pool.partition_all_reduce(amax_all[:, m:m + 1], amax[:, m:m + 1], P, REDUCE_MAX) \
                    .then_inc(pool_step, 1)
                pool.wait_ge(pool_step, n)
                pool.tensor_tensor(amax_all[:, m:m + 1], amax_all[:, m:m + 1], half[:, 0:1], ALU.pow) \
                    .then_inc(attn_bounded, 1)

            rstd_of(0)
            attn_bound(K)
            weight_max(0, V, V + 1)
            attn_bound(Q)
            weight_max(1, M_SU, M_SU + 1)
            pool.wait_ge(norms_read, 1)
            pool.tensor_tensor(norms[:, :], norms[:, :], half[:, :], ALU.pow).then_inc(norms_ready, 1)
            weight_max(2, M_GATE, M_UP + 1)
            weight_max(3, M_COEF, M_COEF + 1)
            weight_max(4, M_DOWN, M_DOWN + 1)
            pool.wait_ge(max_all_ready, 5)
            pool.tensor_tensor(amax_all[:, M_DOWN:M_DOWN + 1], amax_all[:, M_DOWN:M_DOWN + 1], half[:, 0:1],
                               ALU.pow).then_inc(down_bounded, 1)
            ctx_max_of(0)
            attn_bound(O)
            rstd_of(1)
            with pool.Fori(1, CHUNKS - 1) as c:
                ctx_max_of(c)
                rstd_of(c + 1)
            ctx_max_of(CHUNKS - 1)

        @block.scalar
        def _(act):
            def split_attn(m):
                for k in range(KB):
                    act.activation(w_attn[:, m, HI, k, :], raw_attn[m][:, k, :], ACT.Copy,
                                   scale=s_attn[:, m:m + 1]).then_inc(attn_hi, 1)

            def xt_high(c):
                for k in range(KB):
                    act.wait_ge(xp_done, 4 * c + k + 1)
                    act.activation(xt[:, HI, k, :], ring[k][:, :], ACT.Copy).then_inc(xt_hi, 1)

            def square_attn(m):
                act.wait_ge(attn_raw_loaded[m], 16)
                if m != K:
                    act.wait_ge(attn_squared, SQUARED.index(m))
                act.activation(unkept if m != O else unkept_o, flat_attn(m), ACT.Square, accum_out=amax[:, m:m + 1]) \
                    .then_inc(attn_squared, 1)

            def square(u):
                b, m = UNITS[u]
                act.wait_ge(unit_loaded[u], 16)
                if u >= 2:
                    act.wait_ge(normed, u - 1)
                act.activation(squares[:, u % 2, :, :], ug_raw[:, m, b, :, :], ACT.Square).then_inc(squared, 1)

            def square_down(g):
                act.wait_ge(down_loaded[g], 16)
                if g:
                    act.wait_ge(down_squared, g)
                act.activation(unkept_down, down_raw[:, KB * g:KB * g + KB, :].rearrange("p k n -> p (k n)"),
                               ACT.Square, accum_out=down_sums[:, g:g + 1]).then_inc(down_squared, 1)

            def evict_qkv(c):
                for f in range(KB):
                    for j, m in enumerate((K, V, Q)):
                        n = 3 * f + j
                        bank = ring[n % 4]
                        if is_first(c):
                            if n < len(UNITS):
                                square(n)
                            else:
                                square_down(n - len(UNITS))
                        act.wait_ge(qkv_done, 12 * c + n + 1)
                        unscale = i_attn[:, m:m + 1]
                        if m == V:
                            if not (is_first(c) and f == 0):
                                act.wait_ge(v_used, 4 * c + f)
                            act.activation(v_sb[:, :], bank[:, :], ACT.Identity,
                                           bias=vec[:, BV + f:BV + f + 1], scale=unscale).then_inc(v_evicted, 1)
                            continue
                        e, r, b, done = (e_k, r_k, BK, k_evicted) if m == K else (e_q, r_q, BQ, q_evicted)
                        if not (is_first(c) and f == 0):
                            act.wait_ge(ctx_made, 4 * c + f)
                        act.activation(e[:, :], bank[:, :], ACT.Exp, bias=vec[:, b + f:b + f + 1], scale=unscale)
                        act.activation(r[:, :], bank[:, :], ACT.Relu, bias=vec[:, b + f:b + f + 1],
                                       scale=unscale).then_inc(done, 1)

            def split_part(b, m):
                for k in range(KB):
                    n = part_at(b, m) + k
                    act.wait_ge(hada_done, n + 1)
                    bank = early_bank(n) if b < EARLY else ring[k]
                    act.activation(ug[:, m, b, k, HI, :], bank[:, :], ACT.Copy,
                                   scale=coef_ug[:, m, k:k + 1]).then_inc(ffn_hi, 1)

            def silu_gates(c):
                first = is_first(c)
                for i in range(NI):
                    if first and i in (1, 2):
                        split_part(1, i - 1)
                    if first and i == 6:
                        act.wait_ge(coef_ready, 6)
                        split_down(0)
                    if first and i == 7:
                        split_down(1)
                        split_down(2)
                        split_down(3)
                    if first and i == AHEAD:
                        split_part(2, GATE)
                        split_part(2, UP)
                    act.wait_ge(gate_done, 16 * c + i + 1)
                    if not (is_first(c) and i < 2):
                        act.wait_ge(up_read, 16 * c + i - 1)
                    act.activation(silu[:, i % 2, :], ring[(12 + 2 * i) % 4][:, :], ACT.Silu,
                                   scale=gate_out[:, i:i + 1]).then_inc(silu_ready, 1)
                    if first and i > AHEAD and i % 4 in (1, 2) and i // 4 < BLOCKS - 1:
                        split_part(i // 4 + 1, i % 4 - 1)
                    if first and i == 8:
                        square_attn(O)
                    if first and i == 12:
                        act.wait_ge(coef_ready, 7)
                        split_attn(O)

            def silu_outs(c):
                for t in range(TB):
                    act.wait_ge(z_ready, 4 * c + t + 1)
                    act.activation(gate_g[:, t % 2, :], gate_g[:, t % 2, :], ACT.Silu).then_inc(gate_ready, 1)

            def split_down(g):
                for k in range(KB * g, KB * g + KB):
                    act.wait_ge(hada_done, DOWN_AT + k + 1)
                    act.activation(down[:, k, HI, :], early_bank(DOWN_AT + k)[:, :], ACT.Copy,
                                   scale=coef_down[:, k:k + 1]).then_inc(ffn_hi, 1)

            square_attn(K)
            xt_high(0)
            for m in (K, V, Q):
                act.wait_ge(coef_ready, m + 1)
                split_attn(m)
                if m == K:
                    square_attn(Q)
            act.wait_ge(consts_loaded, 48)
            evict_qkv(0)
            act.wait_ge(coef_ready, 4)
            split_part(0, GATE)
            split_part(0, UP)
            act.wait_ge(coef_ready, 5)
            silu_gates(0)
            xt_high(1)
            silu_outs(0)
            with act.Fori(1, CHUNKS - 1) as c:
                evict_qkv(c)
                silu_gates(c)
                xt_high(c + 1)
                silu_outs(c)
            evict_qkv(CHUNKS - 1)
            silu_gates(CHUNKS - 1)
            silu_outs(CHUNKS - 1)

        @block.vector
        def _(dve):
            class Chain:

                def __init__(self, counter, base):
                    self.counter, self.base, self.n = counter, base, 0

                def after(self, ins):
                    self.n += 1
                    ins.then_inc(self.counter, 1)
                    dve.wait_ge(self.counter, self.base + self.n)

            prep = Chain(prep_step, 0)

            def pow2(chain, src, factor, scale, inverse, least=TINY):
                t = pw[:, 0:src.free_size()]
                chain.after(dve.tensor_scalar(t, src, factor, None, ALU.mult))
                chain.after(dve.tensor_scalar(t.bitcast(I32), t.bitcast(I32), EXPONENT, None, ALU.bitwise_and))
                chain.after(dve.tensor_scalar(inverse.bitcast(I32), t.bitcast(I32), float(least << 23),
                                              -float(TOP << 23), ALU.max, ALU.add))
                chain.after(dve.tensor_scalar(scale.bitcast(I32), inverse.bitcast(I32), -1.0,
                                              float(254 << 23), ALU.mult, ALU.add))

            def absmax(dst, src):
                return dve.tensor_reduce(dst, src, AX_X, ALU.max, apply_absolute_value=True)

            def flat(ap):
                return ap.rearrange("p k n -> p (k n)")

            def ln_stats(c, chain):
                if not is_first(c):
                    dve.wait_ge(x_ln_loaded, 16 * c)
                for t in range(TB):
                    if is_first(c):
                        dve.wait_ge(x_first_loaded[t], 16)
                    last = dve.bn_stats(stats[:, t, :], x_ln[:, t, :])
                chain.after(last)
                dve.sem_inc(dve_passed, 1)
                for t in range(TB):
                    last = dve.bn_aggr(mean_var[:, t, :], stats[:, t, :])
                chain.after(last)
                dve.tensor_scalar(var_eps[:, :], mean_var[:, :, 1], EPS, None, ALU.add).then_inc(var_ready, 1)

            def ln_scale(c, chain):
                dve.wait_ge(rstd_ready, c + 1)
                chain.after(dve.tensor_scalar(rstd[:, :], rstd[:, :], X_SCALE, None, ALU.mult))

            def normalise(t):
                dve.tensor_scalar(x_ln[:, t, :], x_ln[:, t, :], mean_var[:, t, 0:1], rstd[:, t:t + 1],
                                  ALU.subtract, ALU.mult).then_inc(xn_ready, 1)

            def xt_low(c):
                for k in range(KB):
                    dve.wait_ge(xt_hi, 4 * c + k + 1)
                    dve.tensor_tensor(xt[:, LO, k, :], ring[k][:, :], xt[:, HI, k, :], ALU.subtract) \
                        .then_inc(xt_ready, 1)

            def attention(c, chain, between=()):
                for f in range(KB):
                    if 0 < f <= len(between):
                        between[f - 1]()
                    dve.wait_ge(k_evicted, 4 * c + f + 1)
                    chain.after(dve.scalar_tensor_tensor(e_k[:, :], e_k[:, :], 1.0, r_k[:, :], ALU.min, ALU.add))
                    dve.wait_ge(v_evicted, 4 * c + f + 1)
                    dve.tensor_tensor(e_k[:, :], e_k[:, :], v_sb[:, :], ALU.mult).then_inc(v_used, 1)
                    dve.wait_ge(v_used, 4 * c + f + 1)
                    dve.tensor_tensor_scan(r_k[:, :], e_k[:, :], e_k[:, :], 0.0, ALU.add, ALU.bypass)
                    dve.wait_ge(q_evicted, 4 * c + f + 1)
                    chain.after(dve.scalar_tensor_tensor(e_q[:, :], e_q[:, :], 1.0, r_q[:, :], ALU.min, ALU.add))
                    dve.tensor_tensor(ctx_f[:, f, :], e_q[:, :], r_k[:, :], ALU.mult).then_inc(ctx_made, 1)
                    if not between:
                        ctx_absmax(c, f, chain)
                if not between:
                    ctx_absmax_all(chain)

            def ctx_absmax(c, f, chain):
                dve.wait_ge(ctx_made, 4 * c + f + 1)
                chain.after(absmax(ctx_max[:, f:f + 1], ctx_f[:, f, :]))

            def ctx_absmax_all(chain):
                dve.tensor_reduce(ctx_max[:, KB:KB + 1], ctx_max[:, 0:KB], AX_X, ALU.max).then_inc(ctx_max_ready, 1)

            def ctx_scale(c, chain):
                dve.wait_ge(ctx_max_all_ready, c + 1)
                pow2(chain, ctx_max_all[:, 0:1], 1.0, s_c[:, :], i_c[:, :])
                if not is_first(c):
                    take_back_o(chain)

            def take_back_o(chain):
                chain.after(dve.tensor_scalar(o_out[:, :], i_c[:, :], i_attn[:, O:O + 1], HEAD_DIM ** -0.5,
                                              ALU.mult, ALU.mult))

            def split_ctx(f, chain):
                chain.after(dve.tensor_scalar(ctx_s[:, HI, f, :], ctx_f[:, f, :], s_c[:, 0:1], None, ALU.mult))
                dve.scalar_tensor_tensor(ctx_s[:, LO, f, :], ctx_f[:, f, :], s_c[:, 0:1], ctx_s[:, HI, f, :],
                                         ALU.mult, ALU.subtract).then_inc(ctx_split, 1)

            def hidden(c, i, chain):
                dve.wait_ge(silu_ready, 16 * c + i + 1)
                dve.wait_ge(up_done, 16 * c + i + 1)
                if not (is_first(c) and i == 0):
                    dve.wait_ge(h_ready, 16 * c + i)
                dve.scalar_tensor_tensor(h_f, ring[(13 + 2 * i) % 4][:, :], up_out[:, i:i + 1], silu[:, i % 2, :],
                                         ALU.mult, ALU.mult).then_inc(up_read, 1)
                dve.wait_ge(up_read, 16 * c + i + 1)
                h = h_slot(c, i)
                if not (is_first(c) and i < KB + 2):
                    dve.wait_ge(down_step, 16 * c + i - 1)
                chain.after(dve.tensor_copy(h[:, HI, :], h_f))
                dve.tensor_tensor(h[:, LO, :], h_f, h[:, HI, :], ALU.subtract).then_inc(h_ready, 1)

            def gate_argument(c, t):
                if t == 0:
                    dve.wait_ge(down_step, 16 * c + 16)
                dve.scalar_tensor_tensor(gate_g[:, t % 2, :], down_ps[t][:, :], i_d[:, 0:1], ws_dp_row,
                                         ALU.mult, ALU.mult).then_inc(z_ready, 1)

            def outputs(c, chain):
                gate_argument(c, 0)
                gate_argument(c, 1)
                for t in range(TB):
                    dve.wait_ge(o_done, 4 * c + t + 1)
                    if not (is_first(c) and t == 0):
                        dve.wait_ge(out_ready, 4 * c + t)
                    dve.scalar_tensor_tensor(s_f, ring[t][:, :], o_out[:, 0:1], bo_row, ALU.mult, ALU.add) \
                        .then_inc(o_read, 1)
                    dve.wait_ge(o_read, 4 * c + t + 1)
                    dve.wait_ge(gate_ready, 4 * c + t + 1)
                    chain.after(dve.tensor_tensor(s_f, s_f, gate_g[:, t % 2, :], ALU.mult))
                    if t + 2 < TB:
                        gate_argument(c, t + 2)
                    if t == 0:
                        dve.wait_ge(x_res_loaded, 16 * c + 16)
                    dve.tensor_tensor(x_res[:, t, :], x_res[:, t, :], s_f, ALU.add).then_inc(out_ready, 1)

            def feed_forward(c, chain, last):
                for i in range(NI):
                    hidden(c, i, chain)
                    if i == 1:
                        ctx_scale(c, chain)
                    if 2 <= i < 2 + KB:
                        split_ctx(i - 2, chain)
                    if not last and i == 6:
                        ln_stats(c + 1, chain)
                    if not last and i == 8:
                        ln_scale(c + 1, chain)
                    if not last and 9 <= i < 9 + TB:
                        normalise(i - 9)
                if not last:
                    xt_low(c + 1)
                outputs(c, chain)

            def first_feed_forward(chain):
                for i in range(AHEAD, NI):
                    hidden(0, i, chain)
                    if i % 4 in (1, 2) and i // 4 < BLOCKS - 1:
                        split_part(i // 4 + 1, i % 4 - 1)
                    if i == 10:
                        ctx_scale(0, chain)
                    if i == 10:
                        ln_stats(1, chain)
                    if i == 11:
                        prepare_o()
                        ln_scale(1, chain)
                    if 11 <= i < 11 + KB:
                        split_ctx(i - 11, chain)
                    if i == 12:
                        split_attn(O)
                    if i >= 12:
                        normalise(i - 12)
                xt_low(1)
                outputs(0, chain)

            def weight_scale(m):
                if m == V:
                    dve.wait_ge(max_all_ready, 1)
                else:
                    dve.wait_ge(attn_bounded, SQUARED.index(m) + 1)
                pow2(prep, amax_all[:, m:m + 1], MARGIN, s_attn[:, m:m + 1], i_attn[:, m:m + 1], TINY_ROOT)
                dve.tensor_scalar(i_attn[:, m:m + 1], i_attn[:, m:m + 1], 1.0 if m == O else 1.0 / X_SCALE,
                                  None, ALU.mult).then_inc(coef_ready, 1)

            def split_attn(m):
                for k in range(KB):
                    dve.wait_ge(attn_hi, 4 * m + k + 1)
                    dve.scalar_tensor_tensor(w_attn[:, m, LO, k, :], raw_attn[m][:, k, :], s_attn[:, m:m + 1],
                                             w_attn[:, m, HI, k, :], ALU.mult, ALU.subtract).then_inc(attn_split, 1)

            def prepare_o():
                weight_scale(O)
                dve.wait_ge(coef_ready, 7)
                take_back_o(prep)

            def butterfly(src, dst, half):
                a = src.rearrange("p (a two b) n -> p a two b n", two=2, b=half)
                d = dst.rearrange("p (a two b) n -> p a two b n", two=2, b=half)
                dve.tensor_tensor(d[:, :, 0], a[:, :, 0], a[:, :, 1], ALU.add)
                return dve.tensor_tensor(d[:, :, 1], a[:, :, 0], a[:, :, 1], ALU.subtract)

            fly_rows = fly.rearrange("p (k n) -> p k n", k=KB)
            fly_cols = fly.rearrange("p (k n) -> p k n", k=NI)

            def fly_columns(g):
                cols = down_raw[:, :, g * P:(g + 1) * P]
                prep.after(butterfly(cols, fly_cols, 4))
                prep.after(butterfly(fly_cols, cols, 8))

            def fly_four(raw, done):
                if done:
                    dve.wait_ge(flown, done)
                prep.after(butterfly(raw, fly_rows, 1))
                butterfly(fly_rows, raw, 2).then_inc(flown, 1)

            def fly_part(b, m):
                fly_four(ug_raw[:, m, b, :, :], part_at(b, m) // KB)

            def fly_down(g):
                fly_four(down_raw[:, KB * g:KB * g + KB, :], 2 * EARLY + g)

            def split_down(g):
                for k in range(KB * g, KB * g + KB):
                    dve.wait_ge(ffn_hi, DOWN_AT + k + 1)
                    dve.scalar_tensor_tensor(down[:, k, LO, :], early_bank(DOWN_AT + k)[:, :], coef_down[:, k:k + 1],
                                             down[:, k, HI, :], ALU.mult, ALU.subtract).then_inc(ffn_split, 1)

            def split_part(b, m):
                for k in range(KB):
                    n = part_at(b, m) + k
                    dve.wait_ge(ffn_hi, n + 1)
                    bank = early_bank(n) if b < EARLY else ring[k]
                    dve.scalar_tensor_tensor(ug[:, m, b, k, LO, :], bank[:, :], coef_ug[:, m, k:k + 1],
                                             ug[:, m, b, k, HI, :], ALU.mult, ALU.subtract).then_inc(ffn_split, 1)

            dve.memset(ones[:, :], 1.0).then_inc(ones_set, 1)
            ln_stats(0, prep)
            ln_scale(0, prep)
            for t in range(TB):
                normalise(t)
            dve.wait_ge(attn_raw_loaded[V], 16)
            absmax(amax[:, V:V + 1], flat_attn(V)).then_inc(max_ready, 1)
            weight_scale(K)
            xt_low(0)
            weight_scale(V)
            split_attn(K)
            split_attn(V)
            weight_scale(Q)
            split_attn(Q)
            dve.wait_ge(consts_loaded, 48)
            absmax(amax[:, M_SU:M_SU + 1], vec[:, SU_UG:SU_UG + KB]).then_inc(max_ready, 1)

            def columns(g):
                if g == 0:
                    dve.wait_ge(down_squared, GROUPS)
                    dve.wait_ge(flown, 2 * EARLY)
                fly_columns(g)

            def part(b, m):
                dve.wait_ge(squared, 2 * b + m + 1)
                fly_part(b, m)

            def read_norms():
                dve.wait_ge(normed, len(UNITS))
                dve.tensor_scalar(norms[:, :], down_ps[0][:, 0:2 * NI], MARGIN, TINY_SQUARE, ALU.mult, ALU.max) \
                    .then_inc(norms_read, 1)

            chain = Chain(dve_step, 0)

            def scale_gate_up():
                read_norms()
                part(1, UP)
                dve.wait_ge(norms_ready, 1)
                dve.tensor_reduce(amax[:, M_GATE:M_UP + 1], norms[:, :].rearrange("p (m i) -> p m i", m=2),
                                  AX_X, ALU.max).then_inc(max_ready, 1)
                dve.wait_ge(max_all_ready, 3)
                prep.after(dve.tensor_scalar(pw[:, 2:4], amax_all[:, M_GATE:M_UP + 1], amax_all[:, M_SU:M_SU + 1],
                                             None, ALU.mult))
                pow2(prep, pw[:, 2:4], D ** 0.5, s_ug[:, :], i_ug[:, :])
                prep.after(dve.tensor_scalar(coef_ug[:, GATE, :], vec[:, SU_UG:SU_UG + KB], s_ug[:, GATE:GATE + 1],
                                             None, ALU.mult))
                dve.tensor_scalar(coef_ug[:, UP, :], vec[:, SU_UG:SU_UG + KB], s_ug[:, UP:UP + 1], None, ALU.mult) \
                    .then_inc(coef_ready, 1)
                dve.wait_ge(coef_ready, 4)

            part(0, GATE)
            attention(0, chain, (lambda: part(0, UP), lambda: part(1, GATE), scale_gate_up))

            split_part(0, GATE)
            prep.after(dve.tensor_tensor(su2[:, :], amax_all[:, M_SU:M_SU + 1], amax_all[:, M_SU:M_SU + 1], ALU.mult))
            prep.after(dve.tensor_tensor(bound[:, :], vec[:, WS_GATE:WS_GATE + NI], vec[:, WS_UP:WS_UP + NI], ALU.mult))
            prep.after(dve.tensor_scalar(bound[:, :], bound[:, :], su2[:, 0:1], float(D), ALU.mult, ALU.mult))
            prep.after(dve.tensor_tensor(bound[:, :], bound[:, :], norms[:, 0:NI], ALU.mult))
            prep.after(dve.tensor_tensor(bound[:, :], bound[:, :], norms[:, NI:2 * NI], ALU.mult))
            pow2(prep, bound[:, :], 1.0, s_h[:, :], i_h[:, :])
            split_part(0, UP)
            for m, dst, w in ((GATE, gate_out, WS_GATE), (UP, up_out, WS_UP)):
                prep.after(dve.tensor_scalar(dst[:, :], vec[:, w:w + NI], i_ug[:, m:m + 1],
                                             D ** -0.5 / X_SCALE, ALU.mult, ALU.mult))
            dve.tensor_tensor(up_out[:, :], up_out[:, :], s_h[:, :], ALU.mult).then_inc(coef_ready, 1)
            prep.after(dve.tensor_tensor(coef_down[:, :], vec[:, SU_DP:SU_DP + NI], i_h[:, :], ALU.mult))
            absmax(amax[:, M_COEF:M_COEF + 1], coef_down[:, :]).then_inc(max_ready, 1)
            columns(0)
            prep.after(dve.tensor_reduce(amax[:, M_DOWN:M_DOWN + 1], down_sums[:, :], AX_X, ALU.add))
            dve.tensor_scalar(amax[:, M_DOWN:M_DOWN + 1], amax[:, M_DOWN:M_DOWN + 1], MARGIN, TINY_SQUARE,
                              ALU.mult, ALU.max).then_inc(max_ready, 1)
            dve.wait_ge(coef_ready, 5)
            hidden(0, 0, chain)
            split_part(1, GATE)
            columns(1)
            hidden(0, 1, chain)
            split_part(1, UP)
            dve.wait_ge(max_all_ready, 4)
            dve.wait_ge(down_bounded, 1)
            prep.after(dve.tensor_tensor(pw[:, 4:5], amax_all[:, M_COEF:M_COEF + 1],
                                         amax_all[:, M_DOWN:M_DOWN + 1], ALU.mult))
            pow2(prep, pw[:, 4:5], (F * P) ** 0.5, s_d[:, :], i_d[:, :])
            prep.after(dve.tensor_scalar(coef_down[:, :], coef_down[:, :], s_d[:, 0:1], None, ALU.mult))
            dve.tensor_scalar(i_d[:, :], i_d[:, :], F ** -0.5, None, ALU.mult).then_inc(coef_ready, 1)
            columns(2)
            hidden(0, 2, chain)
            columns(3)
            hidden(0, 3, chain)
            fly_down(0)
            hidden(0, 4, chain)
            hidden(0, 5, chain)
            fly_down(1)
            split_down(0)
            split_down(1)
            fly_down(2)
            fly_down(3)
            fly_part(2, GATE)
            hidden(0, 6, chain)
            split_down(2)
            split_down(3)
            fly_part(2, UP)
            hidden(0, 7, chain)
            split_part(2, GATE)
            fly_part(3, GATE)
            split_part(2, UP)
            fly_part(3, UP)
            for f in range(KB):
                ctx_absmax(0, f, chain)
            ctx_absmax_all(chain)

            first_feed_forward(chain)
            before = chain.n
            steps = before + 1
            with dve.Fori(1, CHUNKS - 1) as c:
                chain = Chain(dve_step, c * steps - (steps - before))
                attention(c, chain)
                feed_forward(c, chain, False)
                assert chain.n == steps
            chain = Chain(dve_step, (CHUNKS - 1) * steps - (steps - before))
            attention(CHUNKS - 1, chain)
            feed_forward(CHUNKS - 1, chain, True)

        @block.tensor
        def _(pe):
            def product(bank, pairs):
                for n, (lhs, rhs) in enumerate(pairs):
                    mm = pe.matmul(bank[:, :], lhs, rhs, start=(n == 0), stop=(n == len(pairs) - 1))
                return mm

            def transposes(c):
                pe.wait_ge(xn_ready, 4 * c + 4)
                for k in range(KB):
                    if not is_first(c):
                        if k % 2 == 0:
                            pe.wait_ge(silu_ready, 16 * c - 1 + k // 2)
                        else:
                            pe.wait_ge(up_read, 16 * c - 1 + k // 2)
                    for t in range(TB):
                        mm = pe.transpose(ring[k][:, t * P:(t + 1) * P], x_ln[:, t, k * P:(k + 1) * P], ident[:, :])
                    mm.then_inc(xp_done, 1)

            def norm(u):
                b, m = UNITS[u]
                at = m * NI + 4 * b
                pe.wait_ge(squared, u + 1)
                for n in range(4):
                    for k in range(KB):
                        mm = pe.matmul(down_ps[0][:, at + n:at + n + 1], squares[:, u % 2, k, n * P:(n + 1) * P],
                                       ones[:, :], start=(k == 0), stop=(k == KB - 1))
                mm.then_inc(normed, 1)

            def qkv(c, units=()):
                units = list(units)
                if not is_first(c):
                    pe.wait_ge(xt_ready, 4 * c + 4)
                for f in range(KB):
                    for j, m in enumerate((K, V, Q)):
                        n = 3 * f + j
                        if n < 4:
                            if not is_first(c):
                                pe.wait_ge(o_read, 4 * c - 4 + n + 1)
                        else:
                            before = (n - 4) // 3
                            pe.wait_ge((k_evicted, v_evicted, q_evicted)[(n - 4) % 3], 4 * c + before + 1)
                        cols = slice(f * P, (f + 1) * P)
                        for k in range(KB):
                            if is_first(c) and f == 0:
                                if m == K:
                                    pe.wait_ge(xt_ready, k + 1)
                                pe.wait_ge(attn_split, 4 * m + k + 1)
                            w_hi, w_lo = w_attn[:, m, HI, k, cols], w_attn[:, m, LO, k, cols]
                            pe.matmul(ring[n % 4][:, :], w_hi, xt[:, HI, k, :], start=(k == 0), stop=False)
                            pe.matmul(ring[n % 4][:, :], w_hi, xt[:, LO, k, :], start=False, stop=False)
                            mm = pe.matmul(ring[n % 4][:, :], w_lo, xt[:, HI, k, :], start=False, stop=(k == KB - 1))
                        mm.then_inc(qkv_done, 1)
                        if n >= 1 and units:
                            norm(units.pop(0))
                for u in units:
                    norm(u)

            def gate_or_up(c, i, m):
                n = 2 * i + m
                first = is_first(c)
                b = i // 4
                if first and i in (0, KB):
                    pe.wait_ge(ffn_split, part_at(b, m) + KB)
                if first and i == AHEAD - 1:
                    pe.wait_ge(ffn_split, DOWN_AT + NI - KB + 2 + m + 1)
                elif first and i == AHEAD + 1:
                    pe.wait_ge(ffn_split, part_at(b, UP) + 2 + m + 1)
                elif first and i >= AHEAD and i % 4 == 0:
                    pe.wait_ge(ffn_split, part_at(b, UP) + (KB if m == UP else 1))
                elif first and i >= AHEAD and i % 4 == 2 and b < BLOCKS - 1:
                    pe.wait_ge(ffn_split, part_at(b + 1, GATE) + m + 1)
                elif first and i >= AHEAD and i % 4 == 3 and b < BLOCKS - 1:
                    pe.wait_ge(ffn_split, part_at(b + 1, UP) + 2 + m + 1)
                elif n < 4:
                    pe.wait_ge((k_evicted, v_evicted, q_evicted)[(8 + n) % 3], 4 * c + (8 + n) // 3 + 1)
                else:
                    pe.wait_ge(silu_ready if m == GATE else up_read, 16 * c + i - 1)
                cols = slice(i % 4 * P, (i % 4 + 1) * P)
                pairs = []
                for k in range(KB):
                    w_hi, w_lo = ug[:, m, i // 4, k, HI, cols], ug[:, m, i // 4, k, LO, cols]
                    pairs += [(w_hi, xt[:, HI, k, :]), (w_hi, xt[:, LO, k, :]), (w_lo, xt[:, HI, k, :])]
                product(ring[(12 + n) % 4], pairs).then_inc(gate_done if m == GATE else up_done, 1)

            def down_product(c, i):
                if i == 0:
                    if is_first(c):
                        pe.wait_ge(ffn_split, DOWN_AT + NI // 2)
                    else:
                        pe.wait_ge(gate_ready, 4 * c)
                if is_first(c) and i >= NI // 2 and i % 4 == 0:
                    pe.wait_ge(ffn_split, DOWN_AT + i + KB)
                pe.wait_ge(h_ready, 16 * c + i + 1)
                h = h_slot(c, i)
                for t in range(TB):
                    cols = slice(t * P, (t + 1) * P)
                    pairs = ((h[:, HI, cols], down[:, i, HI, :]), (h[:, HI, cols], down[:, i, LO, :]),
                             (h[:, LO, cols], down[:, i, HI, :]))
                    for n, (lhs, rhs) in enumerate(pairs):
                        mm = pe.matmul(down_ps[t][:, :], lhs, rhs, start=(i == 0 and n == 0),
                                       stop=(i == NI - 1 and n == 2))
                mm.then_inc(down_step, 1)

            def out_product(c, last):
                pe.wait_ge(ctx_split, 4 * c + 4)
                if is_first(c):
                    pe.wait_ge(attn_split, 16)
                for t in range(TB):
                    if not last:
                        pe.wait_ge(xt_ready, 4 * c + 4 + t + 1)
                    elif t % 2 == 0:
                        pe.wait_ge(silu_ready, 16 * c + 15 + t // 2)
                    else:
                        pe.wait_ge(up_read, 16 * c + 15 + t // 2)
                    cols = slice(t * P, (t + 1) * P)
                    pairs = []
                    for f in range(KB):
                        c_hi, c_lo = ctx_s[:, HI, f, cols], ctx_s[:, LO, f, cols]
                        pairs += [(c_hi, w_attn[:, O, HI, f, :]), (c_hi, w_attn[:, O, LO, f, :]),
                                  (c_lo, w_attn[:, O, HI, f, :])]
                    product(ring[t], pairs).then_inc(o_done, 1)

            def early_hadamard(at, rows):
                pe.wait_ge(flown, at // KB + 1)
                for k in range(KB):
                    if at + k >= 4:
                        pe.wait_ge(ffn_split, at + k - 3)
                    pe.matmul(early_bank(at + k)[:, :], hada[:, :], rows[:, k, :], start=True, stop=True) \
                        .then_inc(hada_done, 1)

            def hadamard(b, m):
                if b < EARLY:
                    early_hadamard(part_at(b, m), ug_raw[:, m, b, :, :])
                    return
                pe.wait_ge(flown, part_at(b, m) // KB + 1)
                for k in range(KB):
                    if m == UP and (b == EARLY or k >= 2):
                        pe.wait_ge(ffn_split, part_at(b, GATE) + k + 1)
                    elif b == EARLY and k < 2:
                        pe.wait_ge(ffn_split, DOWN_AT + NI - KB + k + 1)
                    elif b == EARLY:
                        pe.wait_ge((silu_ready, up_read)[k % 2], AHEAD)
                    else:
                        pe.wait_ge((silu_ready, up_read)[k % 2], 4 * (b - 1) + (2 if m == UP else k // 2) + 1)
                    pe.matmul(ring[k][:, :], hada[:, :], ug_raw[:, m, b, k, :], start=True, stop=True) \
                        .then_inc(hada_done, 1)

            def hadamard_down(g):
                rows = down_raw[:, KB * g:KB * g + KB, :]
                if g < GROUPS // 2:
                    early_hadamard(DOWN_AT + KB * g, rows)
                    return
                pe.wait_ge(flown, 2 * EARLY + g + 1)
                for k in range(KB):
                    if g == GROUPS // 2:
                        pe.wait_ge((silu_ready, up_read)[k % 2], AHEAD - 1 - k // 2)
                    else:
                        pe.wait_ge(ffn_split, DOWN_AT + KB * (g - 1) + k + 1)
                    pe.matmul(ring[k][:, :], hada[:, :], rows[:, k, :], start=True, stop=True).then_inc(hada_done, 1)

            def feed_forward(c, last):
                for i in range(NI):
                    gate_or_up(c, i, GATE)
                    gate_or_up(c, i, UP)
                    if i >= 1:
                        down_product(c, i - 1)
                if not last:
                    transposes(c + 1)
                down_product(c, NI - 1)
                out_product(c, last)

            def first_feed_forward():
                for i in range(AHEAD - 1):
                    gate_or_up(0, i, GATE)
                    gate_or_up(0, i, UP)
                    if i in (0, 1):
                        hadamard(1, i)
                    if i >= 5:
                        hadamard_down(i - 5)
                for i in range(5):
                    down_product(0, i)
                hadamard_down(2)
                down_product(0, 5)
                hadamard_down(3)
                down_product(0, 6)
                gate_or_up(0, 7, GATE)
                gate_or_up(0, 7, UP)
                hadamard(2, GATE)
                down_product(0, 7)
                hadamard(2, UP)
                for i in range(AHEAD, NI):
                    gate_or_up(0, i, GATE)
                    gate_or_up(0, i, UP)
                    if i > AHEAD:
                        down_product(0, i - 1)
                    if i % 4 in (1, 2) and i // 4 < BLOCKS - 1:
                        hadamard(i // 4 + 1, i % 4 - 1)
                transposes(1)
                down_product(0, NI - 1)
                out_product(0, False)

            pe.wait_ge(ident_loaded, 16)
            transposes(0)
            pe.wait_ge(ones_set, 1)
            qkv(0, range(len(UNITS)))
            pe.wait_ge(consts_loaded, 48)
            pe.wait_ge(norms_read, 1)
            hadamard(0, GATE)
            hadamard(0, UP)
            first_feed_forward()
            with pe.Fori(1, CHUNKS - 1) as c:
                qkv(c)
                feed_forward(c, False)
            qkv(CHUNKS - 1)
            feed_forward(CHUNKS - 1, True)


def kernel(**inputs):
    import numpy as np
    import concourse.bacc as bacc
    from concourse.bass_utils import run_bass_kernel_spmd

    def part(name):
        return np.asarray(inputs[name])

    def by_partition(v):
        return np.asarray(v).reshape(-1, P).T

    hadamard = np.ones((1, 1), np.float32)
    while hadamard.shape[0] < P:
        hadamard = np.block([[hadamard, hadamard], [hadamard, -hadamard]])
    ws_ug = part("L0_ffn_Wscale_ug")
    arrays = {
        "x": part("L0_attn_x"),
        "wk_t": part("L0_attn_Wk").T, "wv_t": part("L0_attn_Wv").T, "wq_t": part("L0_attn_Wq").T,
        "wo_t": part("L0_attn_Wo").T,
        "gate_t": part("L0_ffn_W_gate").T, "up_t": part("L0_ffn_W_up").T, "down_t": part("L0_ffn_W_down").T,
        "vecs": np.concatenate([by_partition(v) for v in (
            part("L0_attn_bk"), part("L0_attn_bv"), part("L0_attn_bq"), part("L0_ffn_SU_ug"),
            part("L0_ffn_SU_dp"), ws_ug[F:], ws_ug[:F])], axis=1),
        "rows": np.stack([part("L0_attn_bo"), part("L0_ffn_Wscale_dp")]),
        "ident": np.eye(P, dtype=np.float32),
        "hadamard": hadamard,
    }
    arrays = {f"in_{k}": np.ascontiguousarray(v) for k, v in arrays.items()}
    nc = bacc.Bacc("TRN2", target_bir_lowering=False, num_devices=1)
    args = [nc.dram_tensor(k, v.shape, mybir.dt.from_np(v.dtype), kind="ExternalInput").ap()
            for k, v in arrays.items()]
    args.append(nc.dram_tensor("out", (CHUNKS, T, D), F32, kind="ExternalOutput").ap())
    build(nc, *args)
    r = run_bass_kernel_spmd(nc, [arrays], core_ids=[0])
    return r.results[0]["out"]
```
